# Optimizing a Trainium2 kernel written in Bass

```python
import numpy as np
import jax
import jax.numpy as jnp

def _softmax(x, axis=-1):
    return jax.nn.softmax(x, axis=axis)

def _gelu(x):
    return jax.nn.gelu(x, approximate=True)

def _silu(x):
    return jax.nn.silu(x)

def _sigmoid(x):
    return jax.nn.sigmoid(x)

def _layernorm(x, axis=-1, eps=1e-05):
    m = jnp.mean(x, axis=axis, keepdims=True)
    v = jnp.var(x, axis=axis, keepdims=True)
    return (x - m) / jnp.sqrt(v + eps)

def _scatter_add(tgt, idx, src, axis=0):
    return tgt.at[idx].add(src)

def _segment_sum(src, seg, n):
    return jax.ops.segment_sum(src, seg, n)
kernel_name = 'mk_xattn_seq_d2_seqx_r2_d296aa'

def setup_inputs(seed: int=0):
    np.random.seed(seed)
    _w = jnp.asarray

    def _rec_inputs():
        import jax
        import jax.numpy as jnp
        _rk = jax.random.key(seed)
        x = -0.0002928 + 1 * jax.random.normal(jax.random.fold_in(_rk, 1), (2, 1024, 512), jnp.float32)
        _lenS = 1024 - jax.random.randint(jax.random.fold_in(_rk, 7), (2,), 0, max(1, 1024 // 4) + 1, jnp.int32)
        _lenS2 = 2048 - jax.random.randint(jax.random.fold_in(_rk, 8), (2,), 0, max(1, 2048 // 4) + 1, jnp.int32)
        _ctx_1024P = jax.random.normal(jax.random.fold_in(_rk, 11), (2, 16, 512), jnp.float32)
        _ctx_1024c = jax.random.dirichlet(jax.random.fold_in(_rk, 511), 0.3 * jnp.ones((16,), jnp.float32), (2, 2048))
        _ctx_1024t = jnp.einsum('bsk,bkd->bsd', _ctx_1024c, _ctx_1024P)
        _ctx_1024t = _ctx_1024t * jax.lax.rsqrt(jnp.mean(jnp.square(_ctx_1024t)) + 1e-12) * 0.953939
        ctx_1024 = -1.39393e-06 + 0.999914 * (_ctx_1024t + 0.3 * jax.random.normal(jax.random.fold_in(_rk, 611), (2, 2048, 512), jnp.float32))
        itok_BxS2_4_31999 = jax.random.randint(jax.random.fold_in(_rk, 12), (2, 2048), 4, 16000, jnp.int32)
        _ctxb_2048x64P = jax.random.normal(jax.random.fold_in(_rk, 13), (2, 16, 64), jnp.float32)
        _ctxb_2048x64c = jax.random.dirichlet(jax.random.fold_in(_rk, 513), 0.3 * jnp.ones((16,), jnp.float32), (2, 2048))
        _ctxb_2048x64t = jnp.einsum('bsk,bkd->bsd', _ctxb_2048x64c, _ctxb_2048x64P)
        _ctxb_2048x64t = _ctxb_2048x64t * jax.lax.rsqrt(jnp.mean(jnp.square(_ctxb_2048x64t)) + 1e-12) * 0.953939
        ctxb_2048x64 = 0.50053 + 0.288505 * (_ctxb_2048x64t + 0.3 * jax.random.normal(jax.random.fold_in(_rk, 613), (2, 2048, 64), jnp.float32))
        return (x, ctx_1024, itok_BxS2_4_31999, ctxb_2048x64)
    x, ctx_1024, itok_BxS2_4_31999, ctxb_2048x64 = _rec_inputs()

    def _L0_xattn_setup():
        import jax, jax.numpy as jnp
        import numpy as np
        D = 512
        H = 16
        HD = D // H
        DFF = 4 * D
        LN_EPS = 1e-05

        def layernorm(x, gamma, beta):
            mu = jnp.mean(x, axis=-1, keepdims=True)
            var = jnp.mean(jnp.square(x - mu), axis=-1, keepdims=True)
            return (x - mu) * jax.lax.rsqrt(var + LN_EPS) * gamma + beta
        key = jax.random.key(seed)
        ks = jax.random.split(key, 10)
        B, Nq, Nk = (2, 1024, 1024)
        s = 0.02
        return {'q_x': jax.random.normal(ks[0], (B, Nq, D), jnp.float32), 'kv_x': jax.random.normal(ks[1], (B, Nk, D), jnp.float32), 'Wq': jax.random.normal(ks[2], (D, D), jnp.float32) * s, 'Wkv': jax.random.normal(ks[3], (2 * D, D), jnp.float32) * s, 'Wo': jax.random.normal(ks[4], (D, D), jnp.float32) * s, 'bo': jnp.zeros((D,), jnp.float32), 'ln_q_g': jnp.ones((D,), jnp.float32), 'ln_q_b': jnp.zeros((D,), jnp.float32), 'ln_kv_g': jnp.ones((D,), jnp.float32), 'ln_kv_b': jnp.zeros((D,), jnp.float32), 'W1': jax.random.normal(ks[5], (DFF, D), jnp.float32) * s, 'b1': jnp.zeros((DFF,), jnp.float32), 'W2': jax.random.normal(ks[6], (D, DFF), jnp.float32) * s, 'b2': jnp.zeros((D,), jnp.float32)}
    _L0_xattn_all = _L0_xattn_setup()
    _L0_xattn_in = {k: v for k, v in _L0_xattn_all.items() if k in ('Wq', 'Wkv', 'Wo', 'bo', 'ln_q_g', 'ln_q_b', 'ln_kv_g', 'ln_kv_b', 'W1', 'b1', 'W2', 'b2')}
    del _L0_xattn_all

    def _L1_xattn_setup():
        import jax, jax.numpy as jnp
        import numpy as np
        BATCH, T, H, S, P, NH = (4, 1024, 512, 64, 64, 8)
        HD = H // NH

        def _layernorm(x, g, b):
            mu = jnp.mean(x, axis=-1, keepdims=True)
            var = jnp.mean((x - mu) ** 2, axis=-1, keepdims=True)
            return (x - mu) * jax.lax.rsqrt(var + 1e-05) * g + b

        def _mha(q_in, kv_in, W_qkv, b_qkv, W_o, b_o):
            Wq, Wk, Wv = jnp.split(W_qkv, 3, axis=0)
            bq, bk, bv = jnp.split(b_qkv, 3, axis=0)

            def heads(x, W, b):
                y = x @ W.T + b
                return y.reshape(y.shape[0], y.shape[1], NH, HD).transpose(0, 2, 1, 3)
            q, k, v = (heads(q_in, Wq, bq), heads(kv_in, Wk, bk), heads(kv_in, Wv, bv))
            scores = jnp.einsum('bhqd,bhkd->bhqk', q, k) * (1.0 / np.sqrt(HD))
            attn = jax.nn.softmax(scores, axis=-1)
            out = jnp.einsum('bhqk,bhkd->bhqd', attn, v)
            out = out.transpose(0, 2, 1, 3).reshape(q_in.shape)
            return out @ W_o.T + b_o
        key = jax.random.key(seed)
        ks = jax.random.split(key, 16)
        sH = 1.0 / np.sqrt(H)
        d = {}
        d['builder_state'] = jax.random.normal(ks[0], (BATCH, T, H), jnp.float32)
        d['base_state'] = jax.random.normal(ks[1], (BATCH, T, H), jnp.float32)
        d['input_ids'] = jax.random.randint(ks[2], (BATCH, T), 0, 16000)
        d['program_probs'] = jax.random.uniform(ks[3], (BATCH, T, P), jnp.float32)
        d['A'] = jax.random.normal(ks[4], (S, S), jnp.float32) * (0.5 / np.sqrt(S))
        d['Bmat'] = jax.random.normal(ks[5], (H, S), jnp.float32) * sH
        d['Cmat'] = jax.random.normal(ks[6], (S, H), jnp.float32) * (1.0 / np.sqrt(S))
        d['W_in'] = jax.random.normal(ks[7], (H, H), jnp.float32) * sH
        d['b_in'] = jnp.zeros((H,), jnp.float32)
        d['W_qkv'] = jax.random.normal(ks[8], (3 * H, H), jnp.float32) * sH
        d['b_qkv'] = jnp.zeros((3 * H,), jnp.float32)
        d['W_o'] = jax.random.normal(ks[9], (H, H), jnp.float32) * sH
        d['b_o'] = jnp.zeros((H,), jnp.float32)
        d['W_prog'] = jax.random.normal(ks[10], (H, P), jnp.float32) * (1.0 / np.sqrt(P))
        d['b_prog'] = jnp.zeros((H,), jnp.float32)
        d['g1'] = jnp.ones((H,), jnp.float32)
        d['beta1'] = jnp.zeros((H,), jnp.float32)
        d['g2'] = jnp.ones((H,), jnp.float32)
        d['beta2'] = jnp.zeros((H,), jnp.float32)
        return d
    _L1_xattn_all = _L1_xattn_setup()
    _L1_xattn_in = {k: v for k, v in _L1_xattn_all.items() if k in ('A', 'Bmat', 'Cmat', 'W_in', 'b_in', 'W_qkv', 'b_qkv', 'W_o', 'b_o', 'W_prog', 'b_prog', 'g1', 'beta1', 'g2', 'beta2')}
    del _L1_xattn_all
    return {'x': x, 'ctx_1024': ctx_1024, 'itok_BxS2_4_31999': itok_BxS2_4_31999, 'ctxb_2048x64': ctxb_2048x64, 'L0_xattn_Wq': _L0_xattn_in['Wq'], 'L0_xattn_Wkv': _L0_xattn_in['Wkv'], 'L0_xattn_Wo': _L0_xattn_in['Wo'], 'L0_xattn_bo': _L0_xattn_in['bo'], 'L0_xattn_ln_q_g': _L0_xattn_in['ln_q_g'], 'L0_xattn_ln_q_b': _L0_xattn_in['ln_q_b'], 'L0_xattn_ln_kv_g': _L0_xattn_in['ln_kv_g'], 'L0_xattn_ln_kv_b': _L0_xattn_in['ln_kv_b'], 'L0_xattn_W1': _L0_xattn_in['W1'], 'L0_xattn_b1': _L0_xattn_in['b1'], 'L0_xattn_W2': _L0_xattn_in['W2'], 'L0_xattn_b2': _L0_xattn_in['b2'], 'L1_xattn_A': _L1_xattn_in['A'], 'L1_xattn_Bmat': _L1_xattn_in['Bmat'], 'L1_xattn_Cmat': _L1_xattn_in['Cmat'], 'L1_xattn_W_in': _L1_xattn_in['W_in'], 'L1_xattn_b_in': _L1_xattn_in['b_in'], 'L1_xattn_W_qkv': _L1_xattn_in['W_qkv'], 'L1_xattn_b_qkv': _L1_xattn_in['b_qkv'], 'L1_xattn_W_o': _L1_xattn_in['W_o'], 'L1_xattn_b_o': _L1_xattn_in['b_o'], 'L1_xattn_W_prog': _L1_xattn_in['W_prog'], 'L1_xattn_b_prog': _L1_xattn_in['b_prog'], 'L1_xattn_g1': _L1_xattn_in['g1'], 'L1_xattn_beta1': _L1_xattn_in['beta1'], 'L1_xattn_g2': _L1_xattn_in['g2'], 'L1_xattn_beta2': _L1_xattn_in['beta2']}

def reference(x, ctx_1024, itok_BxS2_4_31999, ctxb_2048x64, L0_xattn_Wq, L0_xattn_Wkv, L0_xattn_Wo, L0_xattn_bo, L0_xattn_ln_q_g, L0_xattn_ln_q_b, L0_xattn_ln_kv_g, L0_xattn_ln_kv_b, L0_xattn_W1, L0_xattn_b1, L0_xattn_W2, L0_xattn_b2, L1_xattn_A, L1_xattn_Bmat, L1_xattn_Cmat, L1_xattn_W_in, L1_xattn_b_in, L1_xattn_W_qkv, L1_xattn_b_qkv, L1_xattn_W_o, L1_xattn_b_o, L1_xattn_W_prog, L1_xattn_b_prog, L1_xattn_g1, L1_xattn_beta1, L1_xattn_g2, L1_xattn_beta2):
    import jax
    import jax.numpy as jnp

    def _L0_xattn_ref(q_x, kv_x, Wq, Wkv, Wo, bo, ln_q_g, ln_q_b, ln_kv_g, ln_kv_b, W1, b1, W2, b2):
        import jax, jax.numpy as jnp
        import numpy as np
        D = 512
        H = 16
        HD = D // H
        DFF = 4 * D
        LN_EPS = 1e-05

        def layernorm(x, gamma, beta):
            mu = jnp.mean(x, axis=-1, keepdims=True)
            var = jnp.mean(jnp.square(x - mu), axis=-1, keepdims=True)
            return (x - mu) * jax.lax.rsqrt(var + LN_EPS) * gamma + beta
        B, Nq, _ = q_x.shape
        Nk = kv_x.shape[1]
        scale = HD ** (-0.5)
        q = layernorm(q_x, ln_q_g, ln_q_b) @ Wq.T
        kv = layernorm(kv_x, ln_kv_g, ln_kv_b) @ Wkv.T
        q = q.reshape(B, Nq, H, HD).transpose(0, 2, 1, 3)
        kv = kv.reshape(B, Nk, 2, H, HD).transpose(2, 0, 3, 1, 4)
        k, v = (kv[0], kv[1])
        attn = jnp.einsum('bhqd,bhkd->bhqk', q, k) * scale
        attn = jax.nn.softmax(attn, axis=-1)
        out = jnp.einsum('bhqk,bhkd->bhqd', attn, v)
        out = out.transpose(0, 2, 1, 3).reshape(B, Nq, D)
        x = q_x + out @ Wo.T + bo
        h = jax.nn.silu(x @ W1.T + b1)
        x = x + h @ W2.T + b2
        return x

    def _L1_xattn_ref(builder_state, base_state, input_ids, program_probs, A, Bmat, Cmat, W_in, b_in, W_qkv, b_qkv, W_o, b_o, W_prog, b_prog, g1, beta1, g2, beta2):
        import jax, jax.numpy as jnp
        import numpy as np
        BATCH, T, H, S, P, NH = (4, 1024, 512, 64, 64, 8)
        HD = H // NH

        def _layernorm(x, g, b):
            mu = jnp.mean(x, axis=-1, keepdims=True)
            var = jnp.mean((x - mu) ** 2, axis=-1, keepdims=True)
            return (x - mu) * jax.lax.rsqrt(var + 1e-05) * g + b

        def _mha(q_in, kv_in, W_qkv, b_qkv, W_o, b_o):
            Wq, Wk, Wv = jnp.split(W_qkv, 3, axis=0)
            bq, bk, bv = jnp.split(b_qkv, 3, axis=0)

            def heads(x, W, b):
                y = x @ W.T + b
                return y.reshape(y.shape[0], y.shape[1], NH, HD).transpose(0, 2, 1, 3)
            q, k, v = (heads(q_in, Wq, bq), heads(kv_in, Wk, bk), heads(kv_in, Wv, bv))
            scores = jnp.einsum('bhqd,bhkd->bhqk', q, k) * (1.0 / np.sqrt(HD))
            attn = jax.nn.softmax(scores, axis=-1)
            out = jnp.einsum('bhqk,bhkd->bhqd', attn, v)
            out = out.transpose(0, 2, 1, 3).reshape(q_in.shape)
            return out @ W_o.T + b_o
        residual = builder_state
        x = _layernorm(builder_state, g1, beta1)
        base_n = _layernorm(base_state, g1, beta1)
        x = residual + _mha(x, base_n, W_qkv, b_qkv, W_o, b_o)
        residual = x
        xn = _layernorm(x, g2, beta2)
        U = (xn @ W_in.T + b_in) @ Bmat

        def step(s, u_t):
            s = jax.nn.silu(s @ A.T) + u_t
            return (s, s)
        _, states = jax.lax.scan(step, jnp.zeros((builder_state.shape[0], S), U.dtype), U.transpose(1, 0, 2))
        ssm_out = jnp.einsum('tbs,sh->bth', states, Cmat)
        x = residual + ssm_out
        mod = program_probs.mean(axis=1) @ W_prog.T + b_prog
        return x + mod[:, None, :]
    x = _L0_xattn_ref(x, ctx_1024, L0_xattn_Wq, L0_xattn_Wkv, L0_xattn_Wo, L0_xattn_bo, L0_xattn_ln_q_g, L0_xattn_ln_q_b, L0_xattn_ln_kv_g, L0_xattn_ln_kv_b, L0_xattn_W1, L0_xattn_b1, L0_xattn_W2, L0_xattn_b2)
    x = _L1_xattn_ref(x, ctx_1024, itok_BxS2_4_31999, ctxb_2048x64, L1_xattn_A, L1_xattn_Bmat, L1_xattn_Cmat, L1_xattn_W_in, L1_xattn_b_in, L1_xattn_W_qkv, L1_xattn_b_qkv, L1_xattn_W_o, L1_xattn_b_o, L1_xattn_W_prog, L1_xattn_b_prog, L1_xattn_g1, L1_xattn_beta1, L1_xattn_g2, L1_xattn_beta2)
    return x

_drawn_inputs = setup_inputs


def setup_inputs(seed=0):
    import zlib

    import numpy as np

    out = dict(_drawn_inputs(seed))
    spreads = {'L0_xattn_bo': (0.0, 0.1),
     'L0_xattn_ln_q_g': (1.0, 0.6),
     'L0_xattn_ln_q_b': (0.0, 0.8),
     'L0_xattn_ln_kv_g': (1.0, 0.6),
     'L0_xattn_ln_kv_b': (0.0, 0.498),
     'L0_xattn_b1': (0.0, 0.1),
     'L0_xattn_b2': (0.0, 0.1),
     'L1_xattn_b_in': (0.0, 0.1),
     'L1_xattn_b_qkv': (0.0, 0.1),
     'L1_xattn_b_o': (0.0, 0.1),
     'L1_xattn_b_prog': (0.0, 0.1),
     'L1_xattn_g1': (1.0, 0.2),
     'L1_xattn_beta1': (0.0, 0.1),
     'L1_xattn_g2': (1.0, 0.2),
     'L1_xattn_beta2': (0.0, 0.1)}
    factors = {'L0_xattn_Wq': 8.0}
    for name, (base, spread) in spreads.items():
        noise = np.random.default_rng([zlib.crc32(name.encode()), seed]).standard_normal(out[name].shape)
        drawn = base * np.exp(spread * noise) if base else spread * noise
        out[name] = jnp.asarray(drawn.astype(out[name].dtype))
    for name, factor in factors.items():
        out[name] = (out[name] * factor).astype(out[name].dtype)
    return out
```

```python
import concourse.bass as bass
from concourse import mybir
from contextlib import ExitStack

F32 = mybir.dt.float32
F32R = mybir.dt.float32r
ALU = mybir.AluOpType
ACT = mybir.ActivationFunctionType
AX = mybir.AxisListType

P = 128
B, NQ, NK, D = 2, 1024, 2048, 512
KC = D // P
DFF = 4 * D
FC = DFF // P
H0, HD0 = 16, 32
H1, HD1 = 8, 64
S = 64
PP = 64
TB = 512
RT = TB // P
QB = NQ // TB
KB = NK // TB
KT = NK // P
EPS = 1e-5

VECTORS = [("ln_q_g", KC), ("ln_q_b", KC), ("ln_kv_g", KC), ("ln_kv_b", KC), ("bo", KC), ("b1", FC), ("b2", KC),
           ("g1", KC), ("beta1", KC), ("g2", KC), ("beta2", KC), ("b_in", KC), ("bq", KC), ("bk", KC), ("bv", KC),
           ("b_o", KC), ("b_prog", KC)]
COL = {}
for _name, _n in VECTORS:
    COL[_name] = sum(n for _, n in COL.values()) if COL else 0
    COL[_name] = (COL[_name], _n)
NCOLS = sum(n for _, n in VECTORS)


class Ctx:

    last = None

    def __init__(self, nc, phase):
        self.nc, self.phase, self.stack = nc, phase, ExitStack()
        self.sems, self.sem_stack = [], ExitStack()

    def __enter__(self):
        self.before = Ctx.last
        return self

    def __exit__(self, *a):
        if self.before:
            self.before[1].close()
        Ctx.last = (self.sems, self.sem_stack)
        return self.stack.__exit__(*a)

    def sb(self, name, shape, dt=F32):
        return self.stack.enter_context(self.nc.sbuf_tensor(f"{self.phase}_{name}", shape, dt))

    def bank(self, name, n=1):
        return self.stack.enter_context(self.nc.psum_tensor(f"{self.phase}_{name}", [P, n * TB], F32))

    def sem(self, name):
        self.sems.append(self.sem_stack.enter_context(self.nc.semaphore(f"{self.phase}_{name}")))
        return self.sems[-1]

    def clear_last(self, pool):
        if self.before:
            for sem in self.before[0]:
                pool.sem_clear(sem)


def wait(eng, sem, value):
    if not isinstance(value, int) or value > 0:
        eng.wait_ge(sem, value)


def wait_apart(eng, sem, value, passed):
    wait(eng, sem, value)
    if not isinstance(value, int):
        eng.sem_inc(passed, 1)


def each(eng, n, body):
    body(0)
    if n > 2:
        with eng.Fori(1, n - 1) as i:
            body(i)
    if n > 1:
        body(n - 1)


def is_last(i, n):
    return isinstance(i, int) and i == n - 1


def split3(pairs_a, pairs_b):
    return [(pairs_a[0], pairs_b[0]), (pairs_a[0], pairs_b[1]), (pairs_a[1], pairs_b[0])]


class Kept:

    def __init__(self, nc, stack):
        def sb(name, shape, dt=F32):
            return stack.enter_context(nc.sbuf_tensor(f"kept_{name}", shape, dt))
        self.ident = sb("ident", [P, P])
        self.ones = sb("ones", [P, P])
        self.halfpow = sb("halfpow", [P, RT])
        self.cols = sb("cols", [P, NCOLS])
        self.bias = sb("bias", [P, 8 * KC])
        self.half_b1 = sb("half_b1", [P, FC])
        self.drive = sb("drive", [P, SL + 1, B, SC])
        self.hist = sb("hist", [S, SL + 1, B, SC])
        self.mod = sb("mod", [P, KC, B])

    def col(self, name, j, n=1):
        first = COL[name][0] + j
        return self.cols[:, first:first + n]

    def bias_of(self, weight, j, n=1):
        first = weight.biascol + j
        return self.bias[:, first:first + n]


def setup(nc, A, K):
    with Ctx(nc, "setup") as c:
        loaded, probs_loaded, cleared, made = c.sem("loaded"), c.sem("probs_loaded"), c.sem("cleared"), c.sem("made")
        wprog = c.sb("wprog", [PP, D])
        probs = c.sb("probs", [PP, B, NK])
        total = c.sb("total", [PP, B])
        mod_ps = c.bank("mod_ps")
        summed, multiplied, mod_done = c.sem("summed"), c.sem("multiplied"), c.sem("mod_done")
        with nc.Block() as block:
            @block.sync
            def _(sp):
                sp.dma_start(K.cols[:, :], A["cols"]).then_inc(loaded, 16)
                sp.dma_start(wprog[:, :], A["wprogT"]).then_inc(loaded, 16)
                sp.dma_start(probs[:, :, :], A["probsT"].rearrange("b p n -> p b n")).then_inc(probs_loaded, 16)

            @block.vector
            def _(dve):
                dve.wait_ge(loaded, 32)
                dve.tensor_scalar(K.half_b1[:, :], K.col("b1", 0, FC), 0.5, None, ALU.mult)
                dve.wait_ge(probs_loaded, 16)
                for b in range(B):
                    dve.tensor_reduce(total[:, b:b + 1], probs[:, b, :], AX.X, ALU.add).then_inc(summed, 1)
                dve.wait_ge(multiplied, KC)
                for m in range(KC):
                    dve.tensor_scalar(K.mod[:, m, :], mod_ps[:, m * B:(m + 1) * B], 1.0 / NK, K.col("b_prog", m),
                                      ALU.mult, ALU.add).then_inc(mod_done, 1)

            @block.tensor
            def _(pe):
                pe.wait_ge(loaded, 32)
                pe.wait_ge(summed, B)
                for m in range(KC):
                    pe.matmul(mod_ps[:, m * B:(m + 1) * B], wprog[:, m * P:(m + 1) * P], total[:, :],
                              start=True, stop=True).then_inc(multiplied, 1)

            @block.gpsimd
            def _(pool):
                c.clear_last(pool)
                pool.memset(K.ident[:, :], 0.0).then_inc(cleared, 1)
                pool.memset(K.ones[:, :], 1.0)
                pool.memset(K.halfpow[:, :], -0.5)
                pool.wait_ge(cleared, 1)
                pool.affine_select(out=K.ident[:, :], in_=K.ident[:, :], compare_op=ALU.not_equal, fill=1.0,
                                   base=0, pattern=[[-1, P]], channel_multiplier=1).then_inc(made, 1)


class Weight:

    def __init__(self, name, src, gain, beta, extra, biascol):
        self.name, self.src, self.gain, self.beta, self.extra, self.biascol = name, src, gain, beta, extra, biascol


def normalize_and_project(nc, phase, K, rows, nblocks, row_weights, col_weights):
    weights = [w for w, *_ in row_weights] + [w for w, *_ in col_weights]
    NW = len(weights)
    groups = [("rows", n, rt) for n in range(len(row_weights)) for rt in range(RT)]
    groups += [("cols", n, m) for n in range(len(col_weights)) for m in range(KC)]
    NG, NR, NM = len(groups), len(row_weights) * RT, len(col_weights) * KC
    RING = 4
    with Ctx(nc, phase) as c:
        w_raw = c.sb("w_raw", [P, 2, KC, D])
        w_hi = [c.sb(f"{w.name}_hi", [P, KC, D], F32R) for w in weights]
        w_lo = [c.sb(f"{w.name}_lo", [P, KC, D], F32R) for w in weights]
        x_in = c.sb("x_in", [P, RT, D])
        x_norm = c.sb("x_norm", [P, RT, D])
        xt_hi = c.sb("xt_hi", [P, KC, TB], F32R)
        xt_lo = c.sb("xt_lo", [P, KC, TB], F32R)
        stats = c.sb("stats", [P, RT, 6])
        mv = c.sb("mv", [P, RT, 2])
        var_eps = c.sb("var_eps", [P, RT])
        rstd = c.sb("rstd", [P, RT])
        out_rows = c.sb("out_rows", [P, RING, D])
        out_hi = c.sb("out_hi", [P, RING, TB], F32R)
        out_lo = c.sb("out_lo", [P, RING, TB], F32R)
        turned = [c.bank(f"turned{i}") for i in range(2)]
        acc = [c.bank(f"acc{i}") for i in range(RING)]
        beta_ps = c.bank("beta_ps")
        w_rounded, w_split, beta_done, bias_kept = (
            c.sem(x) for x in ("w_rounded", "w_split", "beta_done", "bias_kept"))
        w_loaded = [c.sem(f"w_loaded{i}") for i in range(2)]
        x_loaded, stats_done, aggregated, eps_done, rstd_done, norm_done = (
            c.sem(x) for x in ("x_loaded", "stats_done", "aggregated", "eps_done", "rstd_done", "norm_done"))
        turned_done, hi_done, lo_done = (c.sem(x) for x in ("turned_done", "hi_done", "lo_done"))
        acc_done = c.sem("acc_done")
        passed = c.sem("passed")
        rows_ready, hi_ready, lo_ready = c.sem("rows_ready"), c.sem("hi_ready"), c.sem("lo_ready")
        rows_stored = [c.sem(f"rows_stored{i}") for i in range(RING)]
        cols_stored = [c.sem(f"cols_stored{i}") for i in range(RING)]

        with nc.Block() as block:
            @block.sync
            def _(sp):
                for n, w in enumerate(weights):
                    if n >= 2:
                        sp.wait_ge(w_split, n - 1)
                        sp.wait_ge(beta_done, n - 1)
                    sp.dma_start(w_raw[:, n % 2], w.src).then_inc(w_loaded[n % 2], 16)
                sp.dma_start(x_in[:, :, :], rows[0, :, :, :]).then_inc(x_loaded, 16)

                def body(i):
                    if not is_last(i, nblocks):
                        sp.wait_ge(norm_done, RT * i + RT)
                        sp.dma_start(x_in[:, :, :], rows[i + 1, :, :, :]).then_inc(x_loaded, 16)
                    for r in range(NR):
                        _, n, rt = groups[r]
                        sp.wait_ge(rows_ready, NR * i + r + 1)
                        sp.dma_start(row_weights[n][1][i, :, rt, :], out_rows[:, r % RING, :]).then_inc(rows_stored[r % RING], 16)
                    for k in range(NM):
                        _, n, m = groups[NR + k]
                        sp.wait_ge(lo_ready, NM * i + k + 1)
                        sp.dma_start(col_weights[n][1][:, m, i, :], out_hi[:, k % RING, :].bitcast(F32)).then_inc(cols_stored[k % RING], 16)
                        sp.dma_start(col_weights[n][2][:, m, i, :], out_lo[:, k % RING, :].bitcast(F32)).then_inc(cols_stored[k % RING], 16)
                each(sp, nblocks, body)
                for slot in range(RING):
                    if NR:
                        sp.wait_ge(rows_stored[slot], 16 * (NR // RING) * nblocks)
                    sp.wait_ge(cols_stored[slot], 32 * (NM // RING) * nblocks)

            @block.gpsimd
            def _(pool):
                c.clear_last(pool)

                def body(i):
                    wait(pool, norm_done, RT * i)
                    wait_apart(pool, aggregated, RT * i + RT, passed)
                    pool.tensor_scalar(var_eps[:, :], mv[:, :, 1], EPS, None, ALU.add).then_inc(eps_done, 1)
                    pool.wait_ge(eps_done, i + 1)
                    pool.tensor_tensor(rstd[:, :], var_eps[:, :], K.halfpow[:, :], ALU.pow).then_inc(rstd_done, 1)
                each(pool, nblocks, body)

            @block.vector
            def _(dve):
                for n, w in enumerate(weights):
                    dve.wait_ge(w_loaded[n % 2], 16 * (n // 2) + 16)
                    for kc in range(KC):
                        gain = K.col(w.gain, kc)
                        dve.tensor_scalar(w_hi[n][:, kc, :], w_raw[:, n % 2, kc, :], gain, None,
                                          ALU.mult).then_inc(w_rounded, 1)
                    for kc in range(KC):
                        gain = K.col(w.gain, kc)
                        dve.wait_ge(w_rounded, KC * n + kc + 1)
                        ins = dve.scalar_tensor_tensor(out=w_lo[n][:, kc, :], in0=w_raw[:, n % 2, kc, :], scalar=gain,
                                                       in1=w_hi[n][:, kc, :].bitcast(F32), op0=ALU.mult, op1=ALU.subtract)
                    ins.then_inc(w_split, 1)
                for n, w in enumerate(weights):
                    dve.wait_ge(beta_done, NW)
                    kept = K.bias[:, w.biascol:w.biascol + KC]
                    if w.extra is None:
                        dve.tensor_copy(kept, beta_ps[:, KC * n:KC * n + KC]).then_inc(bias_kept, 1)
                    else:
                        dve.tensor_tensor(kept, beta_ps[:, KC * n:KC * n + KC],
                                          K.col(w.extra, 0, KC), ALU.add).then_inc(bias_kept, 1)

                def norm(i):
                    dve.wait_ge(x_loaded, 16 * i + 16)
                    for rt in range(RT):
                        dve.bn_stats(stats[:, rt, :], x_in[:, rt, :]).then_inc(stats_done, 1)
                    for rt in range(RT):
                        wait_apart(dve, stats_done, RT * i + rt + 1, passed)
                        dve.bn_aggr(mv[:, rt, :], stats[:, rt, :]).then_inc(aggregated, 1)
                    dve.wait_ge(rstd_done, i + 1)
                    wait(dve, turned_done, KC * i)
                    for rt in range(RT):
                        dve.tensor_scalar(x_norm[:, rt, :], x_in[:, rt, :], mv[:, rt, 0:1], rstd[:, rt:rt + 1],
                                          ALU.subtract, ALU.mult).then_inc(norm_done, 1)
                norm(0)
                dve.wait_ge(bias_kept, NW)

                def body(i):
                    for kc in range(KC):
                        dve.wait_ge(hi_done, KC * i + kc + 1)
                        dve.tensor_tensor(xt_lo[:, kc, :], turned[kc % 2][:, :], xt_hi[:, kc, :].bitcast(F32),
                                          ALU.subtract).then_inc(lo_done, 1)
                    if not is_last(i, nblocks):
                        norm(i + 1)
                    for k in range(NM):
                        _, n, m = groups[NR + k]
                        dve.wait_ge(hi_ready, NM * i + k + 1)
                        wait(dve, cols_stored[k % RING], 32 * (NM // RING * i + k // RING))
                        dve.scalar_tensor_tensor(out=out_lo[:, k % RING, :], in0=acc[(NR + k) % RING][:, :],
                                                 scalar=K.bias_of(col_weights[n][0], m),
                                                 in1=out_hi[:, k % RING, :].bitcast(F32), op0=ALU.add,
                                                 op1=ALU.subtract).then_inc(lo_ready, 1)
                each(dve, nblocks, body)

            @block.scalar
            def _(act):
                act.wait_ge(bias_kept, NW)

                def body(i):
                    for kc in range(KC):
                        act.wait_ge(turned_done, KC * i + kc + 1)
                        if kc == 0:
                            wait(act, acc_done, NG * i)
                        act.activation(xt_hi[:, kc, :], turned[kc % 2][:, :], ACT.Copy).then_inc(hi_done, 1)
                    for r in range(NR):
                        act.wait_ge(acc_done, NG * i + r + 1)
                        wait(act, rows_stored[r % RING], 16 * (NR // RING * i + r // RING))
                        act.activation(out_rows[:, r % RING, :], acc[r % RING][:, :], ACT.Copy).then_inc(rows_ready, 1)
                    for k in range(NM):
                        _, n, m = groups[NR + k]
                        act.wait_ge(acc_done, NG * i + NR + k + 1)
                        wait(act, cols_stored[k % RING], 32 * (NM // RING * i + k // RING))
                        act.activation(out_hi[:, k % RING, :], acc[(NR + k) % RING][:, :], ACT.Identity,
                                       bias=K.bias_of(col_weights[n][0], m)).then_inc(hi_ready, 1)
                each(act, nblocks, body)

            @block.tensor
            def _(pe):
                for n, w in enumerate(weights):
                    pe.wait_ge(w_loaded[n % 2], 16 * (n // 2) + 16)
                    for m in range(KC):
                        for kc in range(KC):
                            ins = pe.matmul(beta_ps[:, KC * n + m:KC * n + m + 1], w_raw[:, n % 2, kc, m * P:(m + 1) * P],
                                            K.col(w.beta, kc), start=(kc == 0), stop=(kc == KC - 1))
                    ins.then_inc(beta_done, 1)
                pe.wait_ge(w_split, NW)

                def body(i):
                    pe.wait_ge(norm_done, RT * i + RT)
                    for kc in range(KC):
                        if kc >= 2:
                            pe.wait_ge(lo_done, KC * i + kc - 1)
                        else:
                            wait(pe, lo_done, KC * i + kc - 1)
                        for rt in range(RT):
                            ins = pe.transpose(turned[kc % 2][:, rt * P:(rt + 1) * P], x_norm[:, rt, kc * P:(kc + 1) * P],
                                               K.ident[:, :])
                        ins.then_inc(turned_done, 1)
                    pe.wait_ge(lo_done, KC * i + KC)
                    for g, (kind, n, m) in enumerate(groups):
                        if g >= RING:
                            back = g - RING
                            if back < NR:
                                pe.wait_ge(rows_ready, NR * i + back + 1)
                            else:
                                pe.wait_ge(lo_ready, NM * i + back - NR + 1)
                        else:
                            wait(pe, lo_ready, NM * i + g - RING + 1)
                        step = 0
                        for kc in range(KC):
                            if kind == "rows":
                                parts = split3((xt_hi[:, kc, m * P:(m + 1) * P], xt_lo[:, kc, m * P:(m + 1) * P]),
                                               (w_hi[n][:, kc, :], w_lo[n][:, kc, :]))
                            else:
                                nn = len(row_weights) + n
                                parts = split3((w_hi[nn][:, kc, m * P:(m + 1) * P], w_lo[nn][:, kc, m * P:(m + 1) * P]),
                                               (xt_hi[:, kc, :], xt_lo[:, kc, :]))
                            for lhsT, rhs in parts:
                                ins = pe.matmul(acc[g % RING][:, :], lhsT, rhs, start=(step == 0), stop=(step == 3 * KC - 1))
                                step += 1
                        ins.then_inc(acc_done, 1)
                each(pe, nblocks, body)


class Layer:

    def __init__(self, heads, hd, stacks, max_rows, bufs, dve_cols):
        self.heads, self.hd, self.stacks, self.max_rows, self.bufs = heads, hd, stacks, max_rows, bufs
        self.dve_cols = dve_cols
        self.nh = P // hd
        self.scale = hd ** -0.5


LAYER0 = Layer(H0, HD0, [(97, [(0, "hi"), (32, "lo"), (64, "hi")], [(0, "hi"), (32, "hi"), (64, "lo")], 96)], 96, 4, 512)
LAYER1 = Layer(H1, HD1, [(128, [(0, "hi"), (64, "hi")], [(0, "hi"), (64, "lo")], None),
                         (96, [(0, "lo")], [(0, "hi")], 64)], 128, 4, 320)


def attention(nc, phase, K, layer, k, q, v, out, qblocks, v_bias, extra=None):
    NH, HD, QPS, NBUF = layer.nh, layer.hd, len(qblocks), layer.bufs
    NP = NH // 2
    BODY = B * QPS
    NM = NH * RT * KB
    R = NM + 2
    S_UNIT = 3
    CHUNKS = 4
    share = [2 if S_UNIT <= u <= S_UNIT + CHUNKS + 1 else 3 for u in range(KT - 1)] + [0]
    m_upto = [NM * sum(share[:u]) // sum(share) for u in range(KT + 1)]
    NBLK = KC * BODY
    NLOAD = sum(len(kp) + len(qp) for _, kp, qp, _ in layer.stacks)
    QC = QPS * TB
    parts = {"hi": 0, "lo": 1}
    WIDTH = NH * TB
    DC = layer.dve_cols
    ADD_AT = NH

    with Ctx(nc, phase) as c:
        k_st = [c.sb(f"k_stack{n}", [rows, B, NH, NK], F32R) for n, (rows, *_) in enumerate(layer.stacks)]
        q_st = [c.sb(f"q_stack{n}", [rows, B, NH, QC], F32R) for n, (rows, *_) in enumerate(layer.stacks)]
        v_sb = c.sb("v", [P, B, KT, P])
        probs = c.sb("probs", [P, NBUF, WIDTH])
        sums = c.sb("sums", [P, 2, WIDTH])
        maxima = c.sb("maxima", [P, NH * RT, KB])
        top = c.sb("top", [P, NH * RT])
        top_row = c.sb("top_row", [NH * RT, P], F32R)
        sums_kept = c.sb("sums_kept", [P, TB])
        recip = c.sb("recip", [P, TB])
        normed = c.sb("normed", [P, TB])
        out_hi = c.sb("out_hi", [P, 2, TB], F32R)
        out_lo = c.sb("out_lo", [P, 2, TB], F32R)
        scores = [c.bank(f"scores{p}", 2) for p in range(2)]
        small = [c.bank(f"small{i}") for i in range(2)]
        outs = [c.bank(f"outs{i}") for i in range(2)]
        passed = c.sem("passed")
        cleared, ready = c.sem("cleared"), c.sem("ready")
        set_loaded = [c.sem(f"set_loaded{b}") for b in range(B)]
        v_loaded = [c.sem(f"v_loaded{b}") for b in range(B)]
        scores_ready, probs_ready, pv_done = c.sem("scores_ready"), c.sem("probs_ready"), c.sem("pv_done")
        sums_dve, sums_pool = c.sem("sums_dve"), c.sem("sums_pool")
        small_full, small_free = c.sem("small_full"), c.sem("small_free")
        top_done, shift_loaded = c.sem("top_done"), c.sem("shift_loaded")
        kept_done, recip_done = c.sem("kept_done"), c.sem("recip_done")
        out_normed, out_rounded, out_ready = c.sem("out_normed"), c.sem("out_rounded"), c.sem("out_ready")
        out_stored = [c.sem(f"out_stored{i}") for i in range(2)]

        def place(j):
            return j // QPS % B, j % QPS

        def use(n, x):
            if isinstance(n, int) and n == 0:
                return NM + 1 + x, (NM + 1 + x) % 2
            return NM + n * R + x, x % 2

        def uses(n):
            found = []
            for u in range(KT):
                if u == KT - 1 and not is_last(n, NBLK):
                    found.append((u, "shift", 0))
                if not is_last(n, NBLK):
                    found += [(u, "max", m) for m in range(m_upto[u], m_upto[u + 1])]
                if u == S_UNIT and not (isinstance(n, int) and n == 0):
                    found.append((u, "sums", 0))
            return found
        SUMS_AT = [kind for _, kind, _ in uses(1)].index("sums")

        def before(g, j):
            return (g, j - 1) if j > 0 else (g - 1, BODY - 1)

        def after(g, j):
            return (g, j + 1) if j < BODY - 1 else (g + 1, 0)

        with nc.Block() as block:
            @block.sync
            def _(sp):
                def load(g, b):
                    for n, (rows, kp, qp, _) in enumerate(layer.stacks):
                        for first, part in kp:
                            src = k[parts[part]][:, g, b * KB:(b + 1) * KB, :].rearrange("(h p) n t -> p h (n t)", p=HD)
                            sp.dma_start(k_st[n][first:first + HD, b].bitcast(F32), src).then_inc(set_loaded[b], 16)
                        for first, part in qp:
                            q0 = b * QB + qblocks[0]
                            src = q[parts[part]][:, g, q0:q0 + QPS, :].rearrange("(h p) n t -> p h (n t)", p=HD)
                            sp.dma_start(q_st[n][first:first + HD, b].bitcast(F32), src).then_inc(set_loaded[b], 16)
                    for n in range(KB):
                        src = v[b * KB + n, :, :, :].rearrange("p t (g d) -> g p t d", g=KC)[g, :, :, :]
                        sp.dma_start(v_sb[:, b, n * RT:(n + 1) * RT, :], src).then_inc(v_loaded[b], 16)

                def shift(j, at):
                    b, qb = place(j)
                    sp.wait_ge(small_free, at + 1)
                    dst = q_st[-1][layer.stacks[-1][3]:layer.stacks[-1][3] + 1, b, :, qb * TB:(qb + 1) * TB]
                    for h in range(NH):
                        sp.dma_start(dst[:, h, :].bitcast(F32).rearrange("o (t c) -> o t c", t=RT),
                                     top_row[h * RT:(h + 1) * RT, :].bitcast(F32)).then_inc(shift_loaded, 16)

                def store(n, j, g):
                    b, qb = place(j)
                    wait_apart(sp, out_ready, n + 1, passed)
                    for part, src in ((0, out_hi), (1, out_lo)):
                        sp.dma_start(out[part][:, g, b * QB + qblocks[qb], :],
                                     src[:, j % 2, :].bitcast(F32)).then_inc(out_stored[j % 2], 16)

                for b in range(B):
                    load(0, b)
                sp.wait_ge(ready, 1)
                shift(0, NM)

                def body(g):
                    for j in range(BODY):
                        n = g * BODY + j
                        b, qb = place(j)
                        first = isinstance(g, int) and g == 0
                        if qb == 0 and b == 0 and not first:
                            sp.wait_ge(pv_done, KT * n)
                            load(g, B - 1)
                        if qb == 0 and b > 0 and not is_last(g, KC):
                            sp.wait_ge(pv_done, KT * n)
                            load(g + 1, b - 1)
                        if j > 0:
                            store(n - 1, j - 1, g)
                        elif not first:
                            store(n - 1, BODY - 1, g - 1)
                        if not is_last(n, NBLK):
                            at = use(n, [kind for _, kind, _ in uses(n)].index("shift"))[0]
                            shift((j + 1) % BODY, at)
                each(sp, KC, body)
                store(NBLK - 1, BODY - 1, KC - 1)
                for i in range(2):
                    sp.wait_ge(out_stored[i], 32 * (NBLK // 2))

            @block.scalar
            def _(act):
                def body(g):
                    for j in range(BODY):
                        n = g * BODY + j
                        for u in range(KT):
                            U = KT * n + u
                            for p in range(NP):
                                act.wait_ge(scores_ready, NP * U + p + 1)
                                if p == 0:
                                    wait(act, pv_done, U - NBUF + 1)
                                    wait(act, sums_dve, U - NBUF + 1)
                                    wait(act, sums_pool, U - NBUF + 1)
                                act.activation(probs[:, U_slot(j, u), 2 * p * TB:2 * (p + 1) * TB], scores[(NP * u + p) % 2][:, :], ACT.Exp,
                                               scale=layer.scale).then_inc(probs_ready, 1)
                            if extra:
                                extra.act(act, n, j, u)

                def U_slot(j, u):
                    return (KT * j + u) % NBUF
                each(act, KC, body)

            @block.gpsimd
            def _(pool):
                c.clear_last(pool)
                rows, shift_row = layer.stacks[-1][0], layer.stacks[-1][3]
                if rows > shift_row + 1:
                    pool.memset(k_st[-1][shift_row:rows].bitcast(F32), 0.0)
                    pool.memset(q_st[-1][shift_row:rows].bitcast(F32), 0.0).then_inc(cleared, 1)
                    pool.wait_ge(cleared, 1)
                pool.memset(k_st[-1][shift_row:shift_row + 1].bitcast(F32), -1.0).then_inc(ready, 1)

                def body(g):
                    for j in range(BODY):
                        n = g * BODY + j
                        for u in range(1, KT):
                            U = KT * n + u
                            pool.wait_ge(probs_ready, NP * (U + 1))
                            acc = sums[:, j % 2, DC:WIDTH]
                            new = probs[:, (KT * j + u) % NBUF, DC:WIDTH]
                            old = acc
                            if u == 1:
                                if not isinstance(n, int) or n >= 2:
                                    pool.wait_ge(small_full, use(n - 1, SUMS_AT)[0] + 1)
                                old = probs[:, (KT * j) % NBUF, DC:WIDTH]
                            else:
                                pool.wait_ge(sums_pool, U)
                            pool.tensor_tensor(acc, old, new, ALU.add).then_inc(sums_pool, 2 if u == 1 else 1)
                each(pool, KC, body)

            @block.vector
            def _(dve):
                def take_max(m, at, slot):
                    dve.wait_ge(small_full, at + 1)
                    dve.tensor_reduce(maxima[:, m // KB, m % KB:m % KB + 1], small[slot][:, :], AX.X,
                                      ALU.max).then_inc(small_free, 1)

                def take_shift(n, at, slot):
                    dve.wait_ge(small_full, at + 1)
                    wait(dve, shift_loaded, 16 * NH * n)
                    dve.tensor_copy(top_row[:, :], small[slot][0:NH * RT, 0:P]).then_inc(small_free, 1)

                def take_top(at):
                    dve.wait_ge(small_free, at)
                    dve.tensor_reduce(top[:, :], maxima[:, :, :], AX.X, ALU.max).then_inc(top_done, 1)

                def keep_sums(n, at, slot):
                    dve.wait_ge(small_full, at + 1)
                    wait(dve, recip_done, CHUNKS * n)
                    dve.tensor_copy(sums_kept[:, :], small[slot][:, :]).then_inc(small_free, 1)
                    dve.wait_ge(small_free, at + 1)
                    dve.sem_inc(kept_done, 1)

                def finish(g, j, step):
                    n, jj = g * BODY + j, j % 2
                    bias = v_bias[:, bass.ds(g, 1)]
                    if step < CHUNKS:
                        cols = slice(step * TB // CHUNKS, (step + 1) * TB // CHUNKS)
                        if step == 0:
                            dve.wait_ge(kept_done, n + 1)
                            wait(dve, out_normed, n)
                        dve.reciprocal(recip[:, cols], sums_kept[:, cols]).then_inc(recip_done, 1)
                    elif step == CHUNKS:
                        dve.wait_ge(recip_done, CHUNKS * (n + 1))
                        dve.wait_ge(pv_done, KT * (n + 1))
                        dve.tensor_tensor(normed[:, :], outs[jj][:, :], recip[:, :], ALU.mult).then_inc(out_normed, 1)
                        dve.wait_ge(out_normed, n + 1)
                        wait(dve, out_stored[jj], 32 * (g * (BODY // 2) + j // 2))
                        dve.tensor_scalar(out_hi[:, jj, :], normed[:, :], bias, None, ALU.add).then_inc(out_rounded, 1)
                    else:
                        dve.wait_ge(out_rounded, n + 1)
                        dve.scalar_tensor_tensor(out=out_lo[:, jj, :], in0=normed[:, :], scalar=bias,
                                                 in1=out_hi[:, jj, :].bitcast(F32), op0=ALU.add,
                                                 op1=ALU.subtract).then_inc(out_ready, 1)

                def add(n, j, u):
                    U = KT * n + u
                    dve.wait_ge(probs_ready, NP * U + -(-DC // (2 * TB)))
                    acc = sums[:, j % 2, 0:DC]
                    old = acc
                    if u == 1:
                        old = probs[:, (KT * j) % NBUF, 0:DC]
                    else:
                        dve.wait_ge(sums_dve, U)
                    dve.tensor_tensor(acc, old, probs[:, (KT * j + u) % NBUF, 0:DC],
                                      ALU.add).then_inc(sums_dve, 2 if u == 1 else 1)

                for m in range(NM):
                    take_max(m, m, m % 2)
                take_top(NM)
                take_shift(0, NM, NM % 2)

                def body(g):
                    for j in range(BODY):
                        n = g * BODY + j
                        for u in range(KT):
                            mine = [(x, kind, m) for x, (unit, kind, m) in enumerate(uses(n)) if unit == u]
                            for i in range(len(mine) + 1):
                                if i == min(len(mine), ADD_AT):
                                    if u > 1:
                                        add(n, j, u - 1)
                                    elif u == 0 and not (isinstance(n, int) and n == 0):
                                        add(n - 1, before(g, j)[1], KT - 1)
                                    if S_UNIT < u <= S_UNIT + CHUNKS + 2 and not (isinstance(n, int) and n == 0):
                                        finish(*before(g, j), u - S_UNIT - 1)
                                if i == len(mine):
                                    break
                                x, kind, m = mine[i]
                                at, slot = use(n, x)
                                if kind == "max":
                                    take_max(m, at, slot)
                                elif kind == "sums":
                                    keep_sums(n - 1, at, slot)
                                else:
                                    take_shift(n + 1, at, slot)
                            if u == KT - 2 and not is_last(n, NBLK):
                                take_top(use(n, [kind for _, kind, _ in uses(n)].index("shift"))[0])
                            if extra:
                                extra.dve(dve, n, j, u)
                each(dve, KC, body)
                last = NBLK - 1
                add(last, BODY - 1, KT - 1)
                keep_sums(last, *use(last, len(uses(last))))
                for step in range(CHUNKS + 2):
                    finish(KC - 1, BODY - 1, step)

            @block.tensor
            def _(pe):
                def product_for_max(g, j, m, at, slot):
                    b, qb = place(j)
                    h, qt, kb = m // KB // RT, m // KB % RT, m % KB
                    if m == 0 and qb == 0:
                        pe.wait_ge(set_loaded[b], 16 * NLOAD * (g + 1))
                    wait(pe, small_free, at - 1)
                    rows = layer.max_rows
                    q0 = qb * TB + qt * P
                    pe.matmul(small[slot][:, :], q_st[0][0:rows, b, h, q0:q0 + P],
                              k_st[0][0:rows, b, h, kb * TB:(kb + 1) * TB], start=True, stop=True).then_inc(small_full, 1)

                def turn_shift(n, at, slot):
                    pe.wait_ge(top_done, n + 1)
                    wait(pe, small_free, at - 1)
                    pe.transpose(small[slot][0:NH * RT, 0:P], top[:, :], K.ident[:, :]).then_inc(small_full, 1)

                def multiply_v(g, j, kt):
                    n, (b, qb) = g * BODY + j, place(j)
                    U = KT * n + kt
                    pe.wait_ge(probs_ready, NP * (U + 1))
                    if kt == 0 and qb == 0:
                        pe.wait_ge(v_loaded[b], 16 * KB * (g + 1))
                    if kt == 0:
                        wait(pe, out_normed, n - 1)
                    for h in range(NH):
                        ins = pe.matmul(outs[j % 2][h * HD:(h + 1) * HD, :], v_sb[:, b, kt, h * HD:(h + 1) * HD],
                                        probs[:, (KT * j + kt) % NBUF, h * TB:(h + 1) * TB], start=(kt == 0), stop=(kt == KT - 1))
                    ins.then_inc(pv_done, 1)

                def multiply_sums(g, j, at, slot):
                    n = g * BODY + j
                    pe.wait_ge(sums_dve, KT * (n + 1))
                    pe.wait_ge(sums_pool, KT * (n + 1))
                    wait(pe, small_free, at - 1)
                    for h in range(NH):
                        ins = pe.matmul(small[slot][h * HD:(h + 1) * HD, :], K.ones[:, 0:HD], sums[:, j % 2, h * TB:(h + 1) * TB],
                                        start=True, stop=True)
                    ins.then_inc(small_full, 1)

                pe.wait_ge(ready, 1)
                for m in range(NM):
                    product_for_max(0, 0, m, m, m % 2)
                turn_shift(0, NM, NM % 2)

                def body(g):
                    for j in range(BODY):
                        n = g * BODY + j
                        b, qb = place(j)
                        for u in range(KT):
                            U = KT * n + u
                            mine = [(x, kind, m) for x, (unit, kind, m) in enumerate(uses(n)) if unit == u]
                            maxes = [(x, m) for x, kind, m in mine if kind == "max"]
                            shifts = [x for x, kind, _ in mine if kind == "shift"]
                            for x in shifts:
                                turn_shift(n + 1, *use(n, x))
                            if u == 0:
                                for x, m in maxes:
                                    product_for_max(*after(g, j), m, *use(n, x))
                                maxes = []
                            for p in range(NP):
                                wait(pe, probs_ready, NP * U + p - 1)
                                if u == 0 and p == 0:
                                    pe.wait_ge(shift_loaded, 16 * NH * (n + 1))
                                for h in (2 * p, 2 * p + 1):
                                    for s, (rows, *_) in enumerate(layer.stacks):
                                        ins = pe.matmul(scores[(NP * u + p) % 2][:, h % 2 * TB:(h % 2 + 1) * TB],
                                                        k_st[s][0:rows, b, h, u * P:(u + 1) * P],
                                                        q_st[s][0:rows, b, h, qb * TB:(qb + 1) * TB],
                                                        start=(s == 0), stop=(s == len(layer.stacks) - 1))
                                    if h == 2 * p + 1:
                                        ins.then_inc(scores_ready, 1)
                                    for x, m in maxes[h:h + 1]:
                                        product_for_max(*after(g, j), m, *use(n, x))
                            if u > 0:
                                multiply_v(g, j, u - 1)
                            elif not (isinstance(n, int) and n == 0):
                                multiply_v(*before(g, j), KT - 1)
                            for x, m in maxes[NH:]:
                                product_for_max(*after(g, j), m, *use(n, x))
                            for x, kind, _ in mine:
                                if kind == "sums":
                                    multiply_sums(*before(g, j), *use(n, x))
                            if extra:
                                extra.pe(pe, n, j, u)
                each(pe, KC, body)
                multiply_v(KC - 1, BODY - 1, KT - 1)
                last = NBLK - 1
                multiply_sums(KC - 1, BODY - 1, *use(last, len(uses(last))))


def project_and_add(nc, phase, K, w_src, a, residual, bias, out):
    NB = B * QB
    RING = 4
    with Ctx(nc, phase) as c:
        w_raw = c.sb("w_raw", [P, KC, D])
        w = (c.sb("w_hi", [P, KC, D], F32R), c.sb("w_lo", [P, KC, D], F32R))
        a_sb = [c.sb(f"a_{x}", [P, 2, KC, TB], F32R) for x in ("hi", "lo")]
        res = c.sb("res", [P, 2, KC, TB])
        res_b = c.sb("res_b", [P, 2, KC, TB])
        y = c.sb("y", [P, RING, TB])
        acc = [c.bank(f"acc{i}") for i in range(RING)]
        w_loaded, w_rounded, w_split = c.sem("w_loaded"), c.sem("w_rounded"), c.sem("w_split")
        loaded = [c.sem(f"loaded{i}") for i in range(2)]
        acc_done, biased, y_ready = c.sem("acc_done"), c.sem("biased"), c.sem("y_ready")
        stored = [c.sem(f"stored{i}") for i in range(RING)]
        with nc.Block() as block:
            @block.sync
            def _(sp):
                sp.dma_start(w_raw[:, :, :], w_src).then_inc(w_loaded, 16)

                def load(i):
                    for part in range(2):
                        sp.dma_start(a_sb[part][:, i % 2].bitcast(F32), a[part][:, :, i, :]).then_inc(loaded[i % 2], 16)
                    sp.dma_start(res[:, i % 2], residual[:, :, i, :]).then_inc(loaded[i % 2], 16)
                load(0)
                load(1)
                for i in range(NB):
                    for m in range(KC):
                        sp.wait_ge(y_ready, KC * i + m + 1)
                        sp.dma_start(out[:, m, i, :], y[:, m, :]).then_inc(stored[m], 16)
                    if i + 2 < NB:
                        load(i + 2)
                for m in range(KC):
                    sp.wait_ge(stored[m], 16 * NB)

            @block.gpsimd
            def _(pool):
                c.clear_last(pool)

            @block.vector
            def _(dve):
                dve.wait_ge(w_loaded, 16)
                for kc in range(KC):
                    dve.tensor_copy(w[0][:, kc, :], w_raw[:, kc, :]).then_inc(w_rounded, 1)
                for kc in range(KC):
                    dve.wait_ge(w_rounded, kc + 1)
                    dve.tensor_tensor(w[1][:, kc, :], w_raw[:, kc, :], w[0][:, kc, :].bitcast(F32),
                                      ALU.subtract).then_inc(w_split, 1)
                for i in range(NB):
                    dve.wait_ge(loaded[i % 2], 48 * (i // 2 + 1))
                    for m in range(KC):
                        dve.tensor_scalar(res_b[:, i % 2, m, :], res[:, i % 2, m, :], bias[:, m:m + 1], None,
                                          ALU.add).then_inc(biased, 1)
                    for m in range(KC):
                        dve.wait_ge(biased, KC * i + m + 1)
                        dve.wait_ge(acc_done, KC * i + m + 1)
                        if i:
                            dve.wait_ge(stored[m], 16 * i)
                        dve.tensor_tensor(y[:, m, :], res_b[:, i % 2, m, :], acc[m][:, :], ALU.add).then_inc(y_ready, 1)

            @block.tensor
            def _(pe):
                pe.wait_ge(w_split, KC)
                for i in range(NB):
                    pe.wait_ge(loaded[i % 2], 48 * (i // 2 + 1))
                    for m in range(KC):
                        if i:
                            pe.wait_ge(y_ready, KC * (i - 1) + m + 1)
                        step = 0
                        for kc in range(KC):
                            for lhsT, rhs in split3((w[0][:, kc, m * P:(m + 1) * P], w[1][:, kc, m * P:(m + 1) * P]),
                                                    (a_sb[0][:, i % 2, kc, :], a_sb[1][:, i % 2, kc, :])):
                                ins = pe.matmul(acc[m][:, :], lhsT, rhs, start=(step == 0), stop=(step == 3 * KC - 1))
                                step += 1
                        ins.then_inc(acc_done, 1)


def feed_forward(nc, phase, K, w1_src, w2_src, x, out):
    NB = B * QB
    LAG = 2
    RING = 3
    with Ctx(nc, phase) as c:
        w1 = (c.sb("w1_hi", [P, KC, DFF], F32R), c.sb("w1_lo", [P, KC, DFF], F32R))
        w2 = (c.sb("w2_hi", [P, FC, D], F32R), c.sb("w2_lo", [P, FC, D], F32R))
        x_sb = c.sb("x", [P, KC, TB])
        xs = (c.sb("x_hi", [P, KC, TB], F32R), c.sb("x_lo", [P, KC, TB], F32R))
        x_b = c.sb("x_b", [P, KC, TB])
        th = c.sb("tanh", [P, 2, TB])
        z = c.sb("z", [P, 2, TB])
        h2 = c.sb("h2", [P, 2, TB])
        hs = (c.sb("h_hi", [P, RING, TB], F32R), c.sb("h_lo", [P, RING, TB], F32R))
        y = x_b
        z_ps = [c.bank(f"z{i}") for i in range(2)]
        y_ps = [c.bank(f"y{i}") for i in range(KC)]
        w_loaded = [c.sem(f"w_loaded{i}") for i in range(2)]
        w_rounded, w_split = c.sem("w_rounded"), c.sem("w_split")
        loaded, x_rounded, x_split, biased = c.sem("loaded"), c.sem("x_rounded"), c.sem("x_split"), c.sem("biased")
        z_done, z_kept, h_done, h_rounded, h_split = (
            c.sem("z_done"), c.sem("z_kept"), c.sem("h_done"), c.sem("h_rounded"), c.sem("h_split"))
        tanh_done = c.sem("tanh_done")
        y_multiplied, y_done, y_ready, stored = c.sem("y_multiplied"), c.sem("y_done"), c.sem("y_ready"), c.sem("stored")
        raw = [x_sb, x_b]
        pieces = [(w1, kc, n) for n in range(KC) for kc in range(KC)] + [(w2, f, 0) for f in range(FC)]
        PER = KC
        NPC = len(pieces) // PER

        def raw_src(q):
            if q < KC:
                return w1_src[:, :, q * D:(q + 1) * D]
            return w2_src[:, (q - KC) * PER:(q - KC + 1) * PER, :]

        with nc.Block() as block:
            @block.sync
            def _(sp):
                for q in range(NPC):
                    if q >= 2:
                        sp.wait_ge(w_split, PER * (q - 1))
                    sp.dma_start(raw[q % 2][:, :, :], raw_src(q)).then_inc(w_loaded[q % 2], 16)
                sp.wait_ge(w_split, PER * NPC)
                sp.dma_start(x_sb[:, :, :], x[:, :, 0, :]).then_inc(loaded, 16)
                for i in range(NB):
                    if i + 1 < NB:
                        sp.wait_ge(x_split, KC * (i + 1))
                        sp.wait_ge(biased, KC * (i + 1))
                        sp.dma_start(x_sb[:, :, :], x[:, :, i + 1, :]).then_inc(loaded, 16)
                    sp.wait_ge(y_ready, KC * (i + 1))
                    sp.dma_start(out[:, :, i, :], y[:, :, :]).then_inc(stored, 16)
                sp.wait_ge(stored, 16 * NB)

            @block.scalar
            def _(act):
                for i in range(NB):
                    for f in range(FC):
                        n = FC * i + f
                        act.wait_ge(z_done, n + 1)
                        if n >= 2:
                            act.wait_ge(h_done, n - 1)
                        act.activation(th[:, n % 2, :], z_ps[n % 2][:, :], ACT.Tanh, bias=K.half_b1[:, f:f + 1],
                                       scale=0.5).then_inc(tanh_done, 1)
                        act.activation(z[:, n % 2, :], z_ps[n % 2][:, :], ACT.Identity,
                                       bias=K.col("b1", f)).then_inc(z_kept, 1)

            @block.gpsimd
            def _(pool):
                c.clear_last(pool)

            @block.vector
            def _(dve):
                for q in range(NPC):
                    dve.wait_ge(w_loaded[q % 2], 16 * (q // 2) + 16)
                    for k in range(PER):
                        w, a, n = pieces[PER * q + k]
                        dve.tensor_copy(w[0][:, a, n * D:(n + 1) * D], raw[q % 2][:, k, :]).then_inc(w_rounded, 1)
                    for k in range(PER):
                        w, a, n = pieces[PER * q + k]
                        dve.wait_ge(w_rounded, PER * q + k + 1)
                        dve.tensor_tensor(w[1][:, a, n * D:(n + 1) * D], raw[q % 2][:, k, :],
                                          w[0][:, a, n * D:(n + 1) * D].bitcast(F32), ALU.subtract).then_inc(w_split, 1)
                for i in range(NB):
                    dve.wait_ge(loaded, 16 * i + 16)
                    if i:
                        dve.wait_ge(z_done, FC * i)
                    for kc in range(KC):
                        dve.tensor_copy(xs[0][:, kc, :], x_sb[:, kc, :]).then_inc(x_rounded, 1)
                    for kc in range(KC):
                        dve.wait_ge(x_rounded, KC * i + kc + 1)
                        dve.tensor_tensor(xs[1][:, kc, :], x_sb[:, kc, :], xs[0][:, kc, :].bitcast(F32),
                                          ALU.subtract).then_inc(x_split, 1)
                    for f in range(FC):
                        if f == KC:
                            if i:
                                dve.wait_ge(stored, 16 * i)
                            for m in range(KC):
                                dve.tensor_scalar(x_b[:, m, :], x_sb[:, m, :], K.col("b2", m), None,
                                                  ALU.add).then_inc(biased, 1)
                        n = FC * i + f
                        dve.wait_ge(tanh_done, n + 1)
                        dve.wait_ge(z_kept, n + 1)
                        if n >= 2:
                            dve.wait_ge(h_split, n - 1)
                        dve.scalar_tensor_tensor(out=h2[:, n % 2, :], in0=th[:, n % 2, :], scalar=1.0, in1=z[:, n % 2, :],
                                                 op0=ALU.add, op1=ALU.mult).then_inc(h_done, 1)
                        dve.wait_ge(h_done, n + 1)
                        if n >= RING:
                            dve.wait_ge(y_multiplied, n - RING + 1)
                        dve.tensor_copy(hs[0][:, n % RING, :], h2[:, n % 2, :]).then_inc(h_rounded, 1)
                        dve.wait_ge(h_rounded, n + 1)
                        dve.tensor_tensor(hs[1][:, n % RING, :], h2[:, n % 2, :], hs[0][:, n % RING, :].bitcast(F32),
                                          ALU.subtract).then_inc(h_split, 1)
                    dve.wait_ge(y_multiplied, FC * (i + 1))
                    dve.wait_ge(biased, KC * (i + 1))
                    for m in range(KC):
                        dve.scalar_tensor_tensor(out=y[:, m, :], in0=y_ps[m][:, :], scalar=0.5, in1=x_b[:, m, :],
                                                 op0=ALU.mult, op1=ALU.add).then_inc(y_ready, 1)

            @block.tensor
            def _(pe):
                pe.wait_ge(w_split, PER * NPC)

                def hidden(n):
                    f = n % FC
                    if n >= 2:
                        pe.wait_ge(z_kept, n - 1)
                    step = 0
                    for kc in range(KC):
                        for lhsT, rhs in split3((w1[0][:, kc, f * P:(f + 1) * P], w1[1][:, kc, f * P:(f + 1) * P]),
                                                (xs[0][:, kc, :], xs[1][:, kc, :])):
                            ins = pe.matmul(z_ps[n % 2][:, :], lhsT, rhs, start=(step == 0), stop=(step == 3 * KC - 1))
                            step += 1
                    ins.then_inc(z_done, 1)

                def down(n):
                    f = n % FC
                    pe.wait_ge(h_split, n + 1)
                    if f == 0 and n:
                        pe.wait_ge(y_ready, KC * (n // FC))
                    for m in range(KC):
                        for s, (lhsT, rhs) in enumerate(split3(
                                (w2[0][:, f, m * P:(m + 1) * P], w2[1][:, f, m * P:(m + 1) * P]),
                                (hs[0][:, n % RING, :], hs[1][:, n % RING, :]))):
                            ins = pe.matmul(y_ps[m][:, :], lhsT, rhs, start=(f == 0 and s == 0), stop=(f == FC - 1 and s == 2))
                    ins.then_inc(y_multiplied, 1)

                for i in range(NB):
                    pe.wait_ge(x_split, KC * (i + 1))
                    for f in range(FC + LAG):
                        if f < FC:
                            hidden(FC * i + f)
                        if f >= LAG:
                            down(FC * i + f - LAG)


SL = 16
SC = NQ // SL
SN = B * SC
ALIKE = 2.0 ** -19


def normalize_features(nc, phase, K, x, gain, beta, w_src, extra, biascol, out, recurrence=None):
    NB = B * QB
    W = P if recurrence else D
    MO = W // P
    with Ctx(nc, phase) as c:
        w_raw = c.sb("w_raw", [P, KC, W])
        w = (c.sb("w_hi", [P, KC, W], F32R), c.sb("w_lo", [P, KC, W], F32R))
        x_sb = c.sb("x", [P, 2, KC, TB])
        centred = c.sb("centred", [P, 2, KC, TB])
        squared = c.sb("squared", [P, KC, TB])
        var_eps = c.sb("var_eps", [P, TB])
        std = c.sb("std", [P, TB])
        rstd = c.sb("rstd", [P, TB])
        xn = c.sb("xn", [P, 2, TB])
        xs = (c.sb("x_hi", [P, KC, TB], F32R), c.sb("x_lo", [P, KC, TB], F32R))
        o_hi = c.sb("o_hi", [P, KC, TB], F32R)
        o_lo = c.sb("o_lo", [P, KC, TB], F32R)
        mean_ps, var_ps, bias_ps = c.bank("mean_ps"), c.bank("var_ps"), c.bank("bias_ps")
        acc = [c.bank(f"acc{i}") for i in range(4)]
        w_loaded, w_made, w_rounded, w_split = c.sem("w_loaded"), c.sem("w_made"), c.sem("w_rounded"), c.sem("w_split")
        bias_done, bias_kept = c.sem("bias_done"), c.sem("bias_kept")
        loaded = [c.sem(f"loaded{i}") for i in range(2)]
        mean_done, centred_done, squared_done, var_done = (
            c.sem("mean_done"), c.sem("centred_done"), c.sem("squared_done"), c.sem("var_done"))
        eps_done, std_done, rstd_done, xn_done, x_rounded, x_split = (
            c.sem("eps_done"), c.sem("std_done"), c.sem("rstd_done"), c.sem("xn_done"), c.sem("x_rounded"), c.sem("x_split"))
        acc_done, hi_ready, lo_ready = c.sem("acc_done"), c.sem("hi_ready"), c.sem("lo_ready")
        stored = [c.sem(f"stored{i}") for i in range(KC)]
        if recurrence:
            w_in = c.sb("w_in", [P, KC, D])
            bmat = c.sb("bmat", [P, KC, S])
            wbt = c.sb("wbt", [S, D])
            side = c.sb("side", [S, P])
            bb = c.sb("bb", [S, 1])
            prep_ps = c.bank("prep_ps")
            made, prep_done = c.sem("made"), c.sem("prep_done")
        bias = K.bias[:, biascol:biascol + MO]

        with nc.Block() as block:
            @block.sync
            def _(sp):
                if recurrence:
                    sp.dma_start(w_in[:, :, :], recurrence["w_in"].rearrange("(c p) i -> p c i", p=P)).then_inc(w_loaded, 16)
                    sp.dma_start(bmat[:, :, :], recurrence["bmat"].rearrange("(c p) s -> p c s", p=P)).then_inc(w_loaded, 16)
                    sp.dma_start(side[:, S:P], recurrence["aT"]).then_inc(w_loaded, 16)
                else:
                    sp.dma_start(w_raw[:, :, :], w_src).then_inc(w_loaded, 16)
                for i in range(NB):
                    if i >= 2:
                        sp.wait_ge(centred_done, KC * (i - 1))
                    sp.dma_start(x_sb[:, i % 2], x[:, :, i, :]).then_inc(loaded[i % 2], 16)
                if not recurrence:
                    for i in range(NB):
                        for m in range(KC):
                            sp.wait_ge(lo_ready, KC * i + m + 1)
                            sp.dma_start(out[0][:, m, i, :], o_hi[:, m, :].bitcast(F32)).then_inc(stored[m], 16)
                            sp.dma_start(out[1][:, m, i, :], o_lo[:, m, :].bitcast(F32)).then_inc(stored[m], 16)
                    for m in range(KC):
                        sp.wait_ge(stored[m], 32 * NB)

            @block.gpsimd
            def _(pool):
                c.clear_last(pool)

            @block.scalar
            def _(act):
                def square(i):
                    for kc in range(KC):
                        act.wait_ge(centred_done, KC * i + kc + 1)
                        if i and kc == 0:
                            act.wait_ge(var_done, i)
                        act.activation(squared[:, kc, :], centred[:, i % 2, kc, :], ACT.Square).then_inc(squared_done, 1)
                square(0)
                for i in range(NB):
                    act.wait_ge(eps_done, i + 1)
                    act.activation(std[:, :], var_eps[:, :], ACT.Sqrt).then_inc(std_done, 1)
                    if i + 1 < NB:
                        square(i + 1)
                    for kc in range(KC):
                        act.wait_ge(xn_done, KC * i + kc + 1)
                        if i and kc == 0:
                            act.wait_ge(acc_done, MO * i)
                        act.activation(xs[0][:, kc, :], xn[:, kc % 2, :], ACT.Copy).then_inc(x_rounded, 1)
                    if i == 0:
                        act.wait_ge(bias_kept, 1)
                    for m in range(MO):
                        act.wait_ge(acc_done, MO * i + m + 1)
                        if recurrence:
                            b, run = i // QB, i % QB * (TB // SL)
                            act.activation(K.drive[:, 1:SL + 1, b, run:run + TB // SL],
                                           acc[i % 4][:, :].rearrange("p (r l) -> p l r", l=SL), ACT.Identity,
                                           bias=bias).then_inc(hi_ready, 1)
                        else:
                            if i:
                                act.wait_ge(stored[m], 32 * i)
                            act.activation(o_hi[:, m, :], acc[m][:, :], ACT.Identity,
                                           bias=bias[:, m:m + 1]).then_inc(hi_ready, 1)

            @block.vector
            def _(dve):
                if recurrence:
                    dve.tensor_copy(side[:, 0:S], K.ident[0:S, 0:S]).then_inc(made, 1)
                    dve.wait_ge(prep_done, 1)
                    dve.tensor_copy(wbt[:, :], prep_ps[0:S, :]).then_inc(made, 1)
                    dve.wait_ge(prep_done, 2)
                    dve.tensor_copy(bb[:, :], bias_ps[0:S, 0:1]).then_inc(made, 1)
                    dve.wait_ge(prep_done, 3)
                    dve.tensor_copy(w_raw[:, :, :], prep_ps[:, :]).then_inc(w_made, 1)
                    dve.wait_ge(w_made, 1)
                else:
                    dve.wait_ge(w_loaded, 16)
                for kc in range(KC):
                    dve.tensor_scalar(w[0][:, kc, :], w_raw[:, kc, :], K.col(gain, kc), None, ALU.mult).then_inc(w_rounded, 1)
                for kc in range(KC):
                    dve.wait_ge(w_rounded, kc + 1)
                    dve.scalar_tensor_tensor(out=w[1][:, kc, :], in0=w_raw[:, kc, :], scalar=K.col(gain, kc),
                                             in1=w[0][:, kc, :].bitcast(F32), op0=ALU.mult,
                                             op1=ALU.subtract).then_inc(w_split, 1)

                def centre(i):
                    dve.wait_ge(loaded[i % 2], 16 * (i // 2 + 1))
                    dve.wait_ge(mean_done, i + 1)
                    if i >= 2:
                        dve.wait_ge(xn_done, KC * (i - 1))
                        dve.wait_ge(squared_done, KC * (i - 1))
                    for kc in range(KC):
                        dve.scalar_tensor_tensor(out=centred[:, i % 2, kc, :], in0=mean_ps[:, :], scalar=-1.0 / D,
                                                 in1=x_sb[:, i % 2, kc, :], op0=ALU.mult, op1=ALU.add).then_inc(centred_done, 1)
                centre(0)
                dve.wait_ge(bias_done, 1)
                if extra is None:
                    dve.tensor_copy(bias, bias_ps[:, 8:8 + MO]).then_inc(bias_kept, 1)
                else:
                    dve.tensor_tensor(bias, bias_ps[:, 8:8 + MO], K.col(extra, 0, MO), ALU.add).then_inc(bias_kept, 1)
                dve.wait_ge(bias_kept, 1)
                for i in range(NB):
                    dve.wait_ge(var_done, i + 1)
                    dve.tensor_scalar(var_eps[:, :], var_ps[:, :], 1.0 / D, EPS, ALU.mult, ALU.add).then_inc(eps_done, 1)
                    dve.wait_ge(std_done, i + 1)
                    dve.reciprocal(rstd[:, :], std[:, :]).then_inc(rstd_done, 1)
                    if i + 1 < NB:
                        centre(i + 1)
                    dve.wait_ge(rstd_done, i + 1)
                    for kc in range(KC):
                        n = KC * i + kc
                        if n >= 2:
                            dve.wait_ge(x_split, n - 1)
                        dve.wait_ge(centred_done, n + 1)
                        dve.tensor_tensor(xn[:, kc % 2, :], centred[:, i % 2, kc, :], rstd[:, :], ALU.mult).then_inc(xn_done, 1)
                        dve.wait_ge(x_rounded, n + 1)
                        dve.tensor_tensor(xs[1][:, kc, :], xn[:, kc % 2, :], xs[0][:, kc, :].bitcast(F32),
                                          ALU.subtract).then_inc(x_split, 1)
                    if not recurrence:
                        for m in range(MO):
                            dve.wait_ge(hi_ready, MO * i + m + 1)
                            if i:
                                dve.wait_ge(stored[m], 32 * i)
                            dve.scalar_tensor_tensor(out=o_lo[:, m, :], in0=acc[m][:, :], scalar=bias[:, m:m + 1],
                                                     in1=o_hi[:, m, :].bitcast(F32), op0=ALU.add,
                                                     op1=ALU.subtract).then_inc(lo_ready, 1)
                if recurrence:
                    dve.wait_ge(hi_ready, NB)
                    dve.tensor_copy(K.drive[:, 0, :, 1:SC], K.drive[:, SL, :, 0:SC - 1])
                    dve.memset(K.drive[:, 0, :, 0:1], 0.0)

            @block.tensor
            def _(pe):
                def mean(i):
                    pe.wait_ge(loaded[i % 2], 16 * (i // 2 + 1))
                    if i:
                        pe.wait_ge(centred_done, KC * i)
                    for kc in range(KC):
                        ins = pe.matmul(mean_ps[:, :], K.ones[:, :], x_sb[:, i % 2, kc, :], start=(kc == 0), stop=(kc == KC - 1))
                    ins.then_inc(mean_done, 1)

                def variance(i):
                    if i:
                        pe.wait_ge(eps_done, i)
                    for kc in range(KC):
                        pe.wait_ge(squared_done, KC * i + kc + 1)
                        ins = pe.matmul(var_ps[:, :], K.ones[:, :], squared[:, kc, :], start=(kc == 0), stop=(kc == KC - 1))
                    ins.then_inc(var_done, 1)

                if recurrence:
                    pe.wait_ge(w_loaded, 48)
                    for oc in range(KC):
                        ins = pe.matmul(prep_ps[0:S, :], bmat[:, oc, :], w_in[:, oc, :], start=(oc == 0), stop=(oc == KC - 1))
                    ins.then_inc(prep_done, 1)
                    for oc in range(KC):
                        ins = pe.matmul(bias_ps[0:S, 0:1], bmat[:, oc, :], K.col("b_in", oc), start=(oc == 0), stop=(oc == KC - 1))
                    ins.then_inc(prep_done, 1)
                    pe.wait_ge(made, 3)
                    for kc in range(KC):
                        ins = pe.matmul(prep_ps[:, kc * P:(kc + 1) * P], wbt[:, kc * P:(kc + 1) * P], side[:, :],
                                        start=True, stop=True)
                    ins.then_inc(prep_done, 1)
                    pe.wait_ge(w_made, 1)
                    for kc in range(KC):
                        pe.matmul(bias_ps[:, 8:9], w_raw[:, kc, :], K.col(beta, kc), start=(kc == 0), stop=False)
                    pe.matmul(bias_ps[:, 8:9], side[:, :], bb[:, :], start=False, stop=True).then_inc(bias_done, 1)
                else:
                    pe.wait_ge(w_loaded, 16)
                    for m in range(MO):
                        for kc in range(KC):
                            ins = pe.matmul(bias_ps[:, 8 + m:9 + m], w_raw[:, kc, m * P:(m + 1) * P], K.col(beta, kc),
                                            start=(kc == 0), stop=(kc == KC - 1))
                    ins.then_inc(bias_done, 1)
                mean(0)
                variance(0)
                pe.wait_ge(w_split, KC)
                for i in range(NB):
                    if i + 1 < NB:
                        mean(i + 1)
                        variance(i + 1)
                    pe.wait_ge(x_split, KC * (i + 1))
                    for m in range(MO):
                        bank = i % 4 if recurrence else m
                        if i and not recurrence:
                            pe.wait_ge(lo_ready, MO * (i - 1) + m + 1)
                        step = 0
                        for kc in range(KC):
                            for lhsT, rhs in split3((w[0][:, kc, m * P:(m + 1) * P], w[1][:, kc, m * P:(m + 1) * P]),
                                                    (xs[0][:, kc, :], xs[1][:, kc, :])):
                                ins = pe.matmul(acc[bank][:, :], lhsT, rhs, start=(step == 0), stop=(step == 3 * KC - 1))
                                step += 1
                        ins.then_inc(acc_done, 1)


def recur(nc, phase, K, aT):
    BK = TB // SN
    with Ctx(nc, phase) as c:
        a_raw = c.sb("a_raw", [S, S])
        a_half = c.sb("a_half", [S, S])
        pick = c.sb("pick", [P, S])
        th = c.sb("tanh", [S, 2, SN])
        differ = c.sb("differ", [S, SN])
        both = c.sb("both", [S, 2])
        excess = c.sb("excess", [S, 1])
        worst = c.sb("worst", [1, 1])
        alike = c.sb("alike", [1, 1], mybir.dt.int32)
        z = c.bank("z", SL // BK)
        flip = c.bank("flip")
        passed = c.sem("passed")
        a_loaded, a_halved, picked = c.sem("a_loaded"), c.sem("a_halved"), c.sem("picked")
        begun, z_done, tanh_done, h_done = c.sem("begun"), c.sem("z_done"), c.sem("tanh_done"), c.sem("h_done")
        checked, excess_done, flipped, told = c.sem("checked"), c.sem("excess_done"), c.sem("flipped"), c.sem("told")
        h = K.hist

        with nc.Block() as block:
            @block.sync
            def _(sp):
                sp.dma_start(a_raw[:, :], aT).then_inc(a_loaded, 16)
                sp.wait_ge(a_loaded, 16)

            @block.vector
            def _(dve):
                dve.wait_ge(a_loaded, 16)
                dve.tensor_scalar(a_half[:, :], a_raw[:, :], 0.5, None, ALU.mult).then_inc(a_halved, 1)
                dve.memset(h[:, 0, :, :], 0.0).then_inc(begun, 1)

                def steps(p):
                    for l in range(SL):
                        dve.wait_ge(tanh_done, SL * p + l + 1)
                        dve.scalar_tensor_tensor(out=h[:, l + 1, :, :], in0=th[:, l % 2, :], scalar=1.0,
                                                 in1=z[0:S, l * SN:(l + 1) * SN], op0=ALU.add,
                                                 op1=ALU.mult).then_inc(h_done, 1)

                def begin(p):
                    dve.wait_ge(h_done, SL * p)
                    dve.tensor_copy(h[:, 0, :, 1:SC], h[:, SL, :, 0:SC - 1]).then_inc(begun, 1)
                steps(0)
                begin(1)
                steps(1)
                dve.wait_ge(h_done, 2 * SL)
                d = differ[:, 0:B * (SC - 1)].rearrange("s (b c) -> s b c", b=B)
                dve.tensor_tensor(d, h[:, SL, :, 0:SC - 1], h[:, 0, :, 1:SC], ALU.subtract).then_inc(checked, 1)
                dve.wait_ge(checked, 1)
                dve.tensor_tensor(d, d, d, ALU.mult).then_inc(checked, 1)
                dve.wait_ge(checked, 2)
                dve.tensor_reduce(both[:, 0:1], differ[:, 0:B * (SC - 1)], AX.X, ALU.max).then_inc(checked, 1)
                dve.wait_ge(checked, 3)
                dve.tensor_tensor(d, h[:, SL, :, 0:SC - 1], h[:, SL, :, 0:SC - 1], ALU.mult).then_inc(checked, 1)
                dve.wait_ge(checked, 4)
                dve.tensor_reduce(both[:, 1:2], differ[:, 0:B * (SC - 1)], AX.X, ALU.max).then_inc(checked, 1)
                dve.wait_ge(checked, 5)
                dve.scalar_tensor_tensor(out=excess[:, :], in0=both[:, 1:2], scalar=-(ALIKE ** 2), in1=both[:, 0:1],
                                         op0=ALU.mult, op1=ALU.add).then_inc(excess_done, 1)
                dve.wait_ge(flipped, 1)
                dve.tensor_reduce(worst[:, :], flip[0:1, 0:S], AX.X, ALU.max).then_inc(checked, 1)
                dve.wait_ge(checked, 6)
                dve.tensor_scalar(alike[:, :], worst[:, :], 0.0, None, ALU.is_le).then_inc(told, 1)
                dve.wait_ge(told, 1)
                same = dve.value_load(alike[0:1, 0:1], min_val=0, max_val=1)
                with dve.If(same < 1):
                    with dve.Fori(2, SC) as p:
                        begin(p)
                        steps(p)

            @block.scalar
            def _(act):
                def steps(p):
                    for l in range(SL):
                        act.wait_ge(z_done, SL * p + l + 1)
                        act.activation(th[:, l % 2, :], z[0:S, l * SN:(l + 1) * SN], ACT.Tanh,
                                       scale=0.5).then_inc(tanh_done, 1)
                steps(0)
                steps(1)
                act.wait_ge(told, 1)
                same = act.value_load(alike[0:1, 0:1], min_val=0, max_val=1)
                with act.If(same < 1):
                    with act.Fori(2, SC) as p:
                        steps(p)

            @block.gpsimd
            def _(pool):
                c.clear_last(pool)
                pool.memset(pick[:, :], 0.0).then_inc(picked, 1)
                pool.wait_ge(picked, 1)
                pool.affine_select(out=pick[:, :], in_=pick[:, :], compare_op=ALU.not_equal, fill=1.0,
                                   base=-S, pattern=[[-1, S]], channel_multiplier=1).then_inc(picked, 1)

            @block.tensor
            def _(pe):
                def steps(p):
                    drive = K.drive[:, 0:SL, :, :].rearrange("p l b c -> p (l b c)")
                    for q in range(SL // BK):
                        wait(pe, h_done, SL * p)
                        ins = pe.matmul(z[0:S, q * TB:(q + 1) * TB], pick[:, :], drive[:, q * TB:(q + 1) * TB],
                                        start=True, stop=True)
                    for l in range(SL):
                        if l == 0:
                            wait_apart(pe, begun, p + 1, passed)
                        else:
                            wait_apart(pe, h_done, SL * p + l, passed)
                        pe.matmul(z[0:S, l * SN:(l + 1) * SN], a_half[:, :], h[:, l, :, :].rearrange("s b c -> s (b c)"),
                                  start=False, stop=True, skip_group_check=True).then_inc(z_done, 1)
                pe.wait_ge(a_halved, 1)
                pe.wait_ge(picked, 2)
                steps(0)
                steps(1)
                pe.wait_ge(excess_done, 1)
                pe.transpose(flip[0:1, 0:S], excess[:, :], K.ident[0:S, 0:S]).then_inc(flipped, 1)
                pe.wait_ge(told, 1)
                same = pe.value_load(alike[0:1, 0:1], min_val=0, max_val=1)
                with pe.If(same < 1):
                    with pe.Fori(2, SC) as p:
                        steps(p)


def give_out(nc, phase, K, cmat, x3, out):
    NB = B * QB
    RING = 4
    with Ctx(nc, phase) as c:
        c_raw = c.sb("c_raw", [S, D])
        c_both = c.sb("c_both", [P, D], F32R)
        c_low = c.sb("c_low", [P, D], F32R)
        states = c.sb("states", [S, B, NQ])
        s_both = c.sb("s_both", [P, B, NQ], F32R)
        x_sb = c.sb("x", [P, 2, KC, TB])
        y = c.sb("y", [P, RING, TB])
        acc = [c.bank(f"acc{i}") for i in range(RING)]
        c_loaded, c_cleared, c_split = c.sem("c_loaded"), c.sem("c_cleared"), c.sem("c_split")
        loaded = [c.sem(f"loaded{i}") for i in range(2)]
        summed, rounded, s_split = c.sem("summed"), c.sem("rounded"), c.sem("s_split")
        acc_done, y_ready = c.sem("acc_done"), c.sem("y_ready")
        stored = [c.sem(f"stored{i}") for i in range(RING)]
        with nc.Block() as block:
            @block.sync
            def _(sp):
                sp.dma_start(c_raw[:, :], cmat).then_inc(c_loaded, 16)

                def load(i):
                    sp.dma_start(x_sb[:, i % 2], x3[:, :, i, :]).then_inc(loaded[i % 2], 16)
                load(0)
                load(1)
                for i in range(NB):
                    for m in range(KC):
                        sp.wait_ge(y_ready, KC * i + m + 1)
                        sp.dma_start(out[:, m, i, :], y[:, m, :]).then_inc(stored[m], 16)
                    if i + 2 < NB:
                        load(i + 2)
                for m in range(KC):
                    sp.wait_ge(stored[m], 16 * NB)

            @block.gpsimd
            def _(pool):
                c.clear_last(pool)
                pool.memset(c_low[S:P, :].bitcast(F32), 0.0).then_inc(c_cleared, 1)

            @block.vector
            def _(dve):
                for b in range(B):
                    dve.scalar_tensor_tensor(out=states[:, b, :].rearrange("s (c l) -> s l c", l=SL),
                                             in0=K.hist[:, 1:SL + 1, b, :], scalar=0.5, in1=K.drive[0:S, 1:SL + 1, b, :],
                                             op0=ALU.mult, op1=ALU.add).then_inc(summed, 1)
                for b in range(B):
                    dve.wait_ge(summed, b + 1)
                    dve.tensor_copy(s_both[0:S, b, :], states[:, b, :]).then_inc(rounded, 1)
                    dve.wait_ge(rounded, b + 1)
                    dve.tensor_tensor(s_both[S:P, b, :], states[:, b, :], s_both[0:S, b, :].bitcast(F32),
                                      ALU.subtract).then_inc(s_split, 1)
                dve.wait_ge(c_loaded, 16)
                dve.tensor_copy(c_both[0:S, :], c_raw[:, :]).then_inc(c_split, 1)
                dve.tensor_copy(c_both[S:P, :], c_raw[:, :]).then_inc(c_split, 1)
                dve.wait_ge(c_split, 1)
                dve.tensor_tensor(c_low[0:S, :], c_raw[:, :], c_both[0:S, :].bitcast(F32), ALU.subtract).then_inc(c_split, 1)
                for i in range(NB):
                    dve.wait_ge(loaded[i % 2], 16 * (i // 2 + 1))
                    for m in range(KC):
                        dve.wait_ge(acc_done, KC * i + m + 1)
                        if i:
                            dve.wait_ge(stored[m], 16 * i)
                        dve.scalar_tensor_tensor(out=y[:, m, :], in0=acc[m][:, :], scalar=K.mod[:, m, i // QB:i // QB + 1],
                                                 in1=x_sb[:, i % 2, m, :], op0=ALU.add, op1=ALU.add).then_inc(y_ready, 1)

            @block.tensor
            def _(pe):
                pe.wait_ge(c_cleared, 1)
                pe.wait_ge(c_split, 3)
                for i in range(NB):
                    b, t0 = i // QB, i % QB * TB
                    pe.wait_ge(s_split, b + 1)
                    for m in range(KC):
                        if i:
                            pe.wait_ge(y_ready, KC * (i - 1) + m + 1)
                        pe.matmul(acc[m][:, :], c_both[:, m * P:(m + 1) * P], s_both[:, b, t0:t0 + TB], start=True, stop=False)
                        pe.matmul(acc[m][:, :], c_low[:, m * P:(m + 1) * P], s_both[:, b, t0:t0 + TB],
                                  start=False, stop=True).then_inc(acc_done, 1)


def build(nc, A):
    def scratch(name, shape, dt=F32):
        return nc.dram_tensor(name, shape, dt, kind="Internal").ap()

    k0_hi, k0_lo = (scratch(f"k0_{x}", [P, KC, B * KB, TB]) for x in ("hi", "lo"))
    k1_hi, k1_lo = (scratch(f"k1_{x}", [P, KC, B * KB, TB]) for x in ("hi", "lo"))
    q0_hi, q0_lo = (scratch(f"q0_{x}", [P, KC, B * QB, TB]) for x in ("hi", "lo"))
    q1_hi, q1_lo, a1_hi, a1_lo = (scratch(n, [P, KC, B * QB, TB]) for n in ("q1_hi", "q1_lo", "a1_hi", "a1_lo"))
    a0_hi, a0_lo = (scratch(f"a0_{x}", [P, KC, B * QB, TB]) for x in ("hi", "lo"))
    x1, x2, x3 = (scratch(f"x{n}", [P, KC, B * QB, TB]) for n in (1, 2, 3))
    v0, v1 = (scratch(f"v{n}", [B * KB, P, RT, D]) for n in range(2))

    def w_view(ap):
        return ap.rearrange("(c p) o -> p c o", p=P)
    wq0 = Weight("wq0", w_view(A["wq0T"]), "ln_q_g", "ln_q_b", None, 0)
    wk0 = Weight("wk0", w_view(A["wkv0T"][:, 0:D]), "ln_kv_g", "ln_kv_b", None, KC)
    wv0 = Weight("wv0", w_view(A["wkv0T"][:, D:2 * D]), "ln_kv_g", "ln_kv_b", None, 2 * KC)
    wk1 = Weight("wk1", w_view(A["wqkv1T"][:, D:2 * D]), "g1", "beta1", "bk", 3 * KC)
    wv1 = Weight("wv1", w_view(A["wqkv1T"][:, 2 * D:3 * D]), "g1", "beta1", "bv", 4 * KC)
    with ExitStack() as stack:
        K = Kept(nc, stack)
        Ctx.last = None
        setup(nc, A, K)
        ctx_rows = A["ctx"].rearrange("b (n t p) d -> (b n) p t d", p=P, t=RT)
        x_rows = A["x"].rearrange("b (n t p) d -> (b n) p t d", p=P, t=RT)
        normalize_and_project(nc, "ctx", K, ctx_rows, B * KB, [(wv0, v0), (wv1, v1)],
                              [(wk0, k0_hi, k0_lo), (wk1, k1_hi, k1_lo)])
        normalize_and_project(nc, "xq", K, x_rows, B * QB, [], [(wq0, q0_hi, q0_lo)])
        attention(nc, "att0", K, LAYER0, (k0_hi, k0_lo), (q0_hi, q0_lo), v0, (a0_hi, a0_lo), list(range(QB)),
                  K.bias_of(wv0, 0, KC))
        project_and_add(nc, "out0", K, w_view(A["wo0T"]), (a0_hi, a0_lo), A["xT"], K.col("bo", 0, KC), x1)
        feed_forward(nc, "ffn", K, w_view(A["w1T"]), w_view(A["w2T"]), x1, x2)
        normalize_features(nc, "q1", K, x2, "g1", "beta1", w_view(A["wqkv1T"][:, 0:D]), "bq", 5 * KC, (q1_hi, q1_lo))
        attention(nc, "att1", K, LAYER1, (k1_hi, k1_lo), (q1_hi, q1_lo), v1, (a1_hi, a1_lo), list(range(QB)),
                  K.bias_of(wv1, 0, KC))
        project_and_add(nc, "out1", K, w_view(A["wo1T"]), (a1_hi, a1_lo), x2, K.col("b_o", 0, KC), x3)
        normalize_features(nc, "drive", K, x3, "g2", "beta2", None, None, 6 * KC, None,
                           recurrence={n: A[n] for n in ("w_in", "bmat", "aT")})
        recur(nc, "recur", K, A["aT"])
        give_out(nc, "give", K, A["cmat"], x3, A["outT"])
        Ctx.last[1].close()


def layout(inputs):
    import numpy as np
    g = {k: np.asarray(v) for k, v in inputs.items()}
    def T(a):
        return np.ascontiguousarray(a.T)
    bqkv = g["L1_xattn_b_qkv"]
    vec = {"ln_q_g": g["L0_xattn_ln_q_g"], "ln_q_b": g["L0_xattn_ln_q_b"], "ln_kv_g": g["L0_xattn_ln_kv_g"],
           "ln_kv_b": g["L0_xattn_ln_kv_b"], "bo": g["L0_xattn_bo"], "b1": g["L0_xattn_b1"], "b2": g["L0_xattn_b2"],
           "g1": g["L1_xattn_g1"], "beta1": g["L1_xattn_beta1"], "g2": g["L1_xattn_g2"], "beta2": g["L1_xattn_beta2"],
           "b_in": g["L1_xattn_b_in"], "bq": bqkv[0:D], "bk": bqkv[D:2 * D], "bv": bqkv[2 * D:3 * D],
           "b_o": g["L1_xattn_b_o"], "b_prog": g["L1_xattn_b_prog"]}
    cols = np.concatenate([vec[name].reshape(n, P) for name, n in VECTORS], axis=0)
    return {
        "x": g["x"], "xT": g["x"].reshape(B * QB, TB, KC, P).transpose(3, 2, 0, 1), "ctx": g["ctx_1024"],
        "probsT": g["ctxb_2048x64"].transpose(0, 2, 1), "cols": T(cols),
        "wq0T": T(g["L0_xattn_Wq"]), "wkv0T": T(g["L0_xattn_Wkv"]), "wo0T": T(g["L0_xattn_Wo"]),
        "w1T": T(g["L0_xattn_W1"]), "w2T": T(g["L0_xattn_W2"]),
        "wqkv1T": T(g["L1_xattn_W_qkv"]), "wo1T": T(g["L1_xattn_W_o"]), "w_in": g["L1_xattn_W_in"],
        "bmat": g["L1_xattn_Bmat"], "aT": T(g["L1_xattn_A"]), "cmat": g["L1_xattn_Cmat"],
        "wprogT": T(g["L1_xattn_W_prog"]),
    }


def kernel(**inputs):
    import numpy as np
    import concourse.bacc as bacc
    from concourse.bass_utils import run_bass_kernel_spmd

    nc = bacc.Bacc("TRN2", target_bir_lowering=False, num_devices=1)
    arrays, A = {}, {}
    for name, a in layout(inputs).items():
        a = np.ascontiguousarray(a)
        arrays[name] = a
        A[name] = nc.dram_tensor(name, a.shape, mybir.dt.from_np(a.dtype), kind="ExternalInput").ap()
    A["outT"] = nc.dram_tensor("outT", (P, KC, B * QB, TB), F32, kind="ExternalOutput").ap()
    build(nc, A)
    r = run_bass_kernel_spmd(nc, [arrays], core_ids=[0])
    return np.ascontiguousarray(r.results[0]["outT"].transpose(2, 3, 1, 0).reshape(B, NQ, D))
```

```python
import concourse.bass as bass
from concourse import mybir
from contextlib import ExitStack

F32 = mybir.dt.float32
F32R = mybir.dt.float32r
ALU = mybir.AluOpType
ACT = mybir.ActivationFunctionType
AX = mybir.AxisListType

P = 128
B, NQ, NK, D = 2, 1024, 2048, 512
KC = D // P
DFF = 4 * D
FC = DFF // P
H0, HD0 = 16, 32
H1, HD1 = 8, 64
S = 64
PP = 64
TB = 512
RT = TB // P
QB = NQ // TB
KB = NK // TB
KT = NK // P
EPS = 1e-5

VECTORS = [("ln_q_g", KC), ("ln_q_b", KC), ("ln_kv_g", KC), ("ln_kv_b", KC), ("bo", KC), ("b1", FC), ("b2", KC),
           ("g1", KC), ("beta1", KC), ("g2", KC), ("beta2", KC), ("b_in", KC), ("bq", KC), ("bk", KC), ("bv", KC),
           ("b_o", KC), ("b_prog", KC)]
COL = {}
for _name, _n in VECTORS:
    COL[_name] = (sum(n for _, n in COL.values()), _n)
NCOLS = sum(n for _, n in VECTORS)


class Ctx:

    last = None

    def __init__(self, nc, phase):
        self.nc, self.phase, self.stack = nc, phase, ExitStack()
        self.sems, self.sem_stack = [], ExitStack()

    def __enter__(self):
        self.before = Ctx.last
        return self

    def __exit__(self, *a):
        if self.before:
            self.before[1].close()
        Ctx.last = (self.sems, self.sem_stack)
        return self.stack.__exit__(*a)

    def sb(self, name, shape, dt=F32):
        return self.stack.enter_context(self.nc.sbuf_tensor(f"{self.phase}_{name}", shape, dt))

    def bank(self, name, n=1):
        return self.stack.enter_context(self.nc.psum_tensor(f"{self.phase}_{name}", [P, n * TB], F32))

    def sem(self, name):
        self.sems.append(self.sem_stack.enter_context(self.nc.semaphore(f"{self.phase}_{name}")))
        return self.sems[-1]

    def clear_last(self, pool):
        if self.before:
            for sem in self.before[0]:
                pool.sem_clear(sem)


def wait(eng, sem, value):
    if not isinstance(value, int) or value > 0:
        eng.wait_ge(sem, value)


def wait_apart(eng, sem, value, passed):
    wait(eng, sem, value)
    if not isinstance(value, int):
        eng.sem_inc(passed, 1)


def each(eng, n, body):
    body(0)
    if n > 2:
        with eng.Fori(1, n - 1) as i:
            body(i)
    if n > 1:
        body(n - 1)


def is_last(i, n):
    return isinstance(i, int) and i == n - 1


def split3(pairs_a, pairs_b):
    return [(pairs_a[0], pairs_b[0]), (pairs_a[0], pairs_b[1]), (pairs_a[1], pairs_b[0])]


class Kept:

    def __init__(self, nc, stack):
        def sb(name, shape, dt=F32):
            return stack.enter_context(nc.sbuf_tensor(f"kept_{name}", shape, dt))
        self.ident = sb("ident", [P, P])
        self.ones = sb("ones", [P, P])
        self.halfpow = sb("halfpow", [P, RT])
        self.cols = sb("cols", [P, NCOLS])
        self.bias = sb("bias", [P, 8 * KC])
        self.half_b1 = sb("half_b1", [P, FC])
        self.drive = sb("drive", [P, SL + 1, B, SC])
        self.hist = sb("hist", [P, SL + 1, B, SC])
        self.mod = sb("mod", [P, KC, B])

    def col(self, name, j, n=1):
        first = COL[name][0] + j
        return self.cols[:, first:first + n]

    def bias_of(self, weight, j, n=1):
        first = weight.biascol + j
        return self.bias[:, first:first + n]


def setup(nc, A, K):
    with Ctx(nc, "setup") as c:
        loaded, probs_loaded, cleared, made = c.sem("loaded"), c.sem("probs_loaded"), c.sem("cleared"), c.sem("made")
        wprog = c.sb("wprog", [PP, D])
        probs = c.sb("probs", [PP, B, NK])
        total = c.sb("total", [PP, B])
        mod_ps = c.bank("mod_ps")
        summed, multiplied, mod_done = c.sem("summed"), c.sem("multiplied"), c.sem("mod_done")
        with nc.Block() as block:
            @block.sync
            def _(sp):
                sp.dma_start(K.cols[:, :], A["cols"]).then_inc(loaded, 16)
                sp.dma_start(wprog[:, :], A["wprogT"]).then_inc(loaded, 16)
                sp.dma_start(probs[:, :, :], A["probsT"].rearrange("b p n -> p b n")).then_inc(probs_loaded, 16)

            @block.vector
            def _(dve):
                dve.wait_ge(loaded, 32)
                dve.tensor_scalar(K.half_b1[:, :], K.col("b1", 0, FC), 0.5, None, ALU.mult)
                dve.wait_ge(probs_loaded, 16)
                for b in range(B):
                    dve.tensor_reduce(total[:, b:b + 1], probs[:, b, :], AX.X, ALU.add).then_inc(summed, 1)
                dve.wait_ge(multiplied, KC)
                for m in range(KC):
                    dve.tensor_scalar(K.mod[:, m, :], mod_ps[:, m * B:(m + 1) * B], 1.0 / NK, K.col("b_prog", m),
                                      ALU.mult, ALU.add).then_inc(mod_done, 1)

            @block.tensor
            def _(pe):
                pe.wait_ge(loaded, 32)
                pe.wait_ge(summed, B)
                for m in range(KC):
                    pe.matmul(mod_ps[:, m * B:(m + 1) * B], wprog[:, m * P:(m + 1) * P], total[:, :],
                              start=True, stop=True).then_inc(multiplied, 1)

            @block.gpsimd
            def _(pool):
                c.clear_last(pool)
                pool.memset(K.ident[:, :], 0.0).then_inc(cleared, 1)
                pool.memset(K.ones[:, :], 1.0)
                pool.memset(K.halfpow[:, :], -0.5)
                pool.wait_ge(cleared, 1)
                pool.affine_select(out=K.ident[:, :], in_=K.ident[:, :], compare_op=ALU.not_equal, fill=1.0,
                                   base=0, pattern=[[-1, P]], channel_multiplier=1).then_inc(made, 1)


class Weight:

    def __init__(self, name, src, gain, beta, extra, biascol):
        self.name, self.src, self.gain, self.beta, self.extra, self.biascol = name, src, gain, beta, extra, biascol


def normalize_and_project(nc, phase, K, rows, nblocks, row_weights, col_weights):
    weights = [w for w, *_ in row_weights] + [w for w, *_ in col_weights]
    NW = len(weights)
    groups = [("rows", n, rt) for n in range(len(row_weights)) for rt in range(RT)]
    groups += [("cols", n, m) for n in range(len(col_weights)) for m in range(KC)]
    NG, NR, NM = len(groups), len(row_weights) * RT, len(col_weights) * KC
    TURN_AT = max(NR, NG // 2)
    RING = 4

    def each_block(eng, body):
        def two(pair):
            for half in range(2):
                body(2 * pair + half, half)
        each(eng, nblocks // 2, two)

    with Ctx(nc, phase) as c:
        w_raw = c.sb("w_raw", [P, 2, KC, D])
        w_hi = [c.sb(f"{w.name}_hi", [P, KC, D], F32R) for w in weights]
        w_lo = [c.sb(f"{w.name}_lo", [P, KC, D], F32R) for w in weights]
        x_in = c.sb("x_in", [P, RT, D])
        x_norm = c.sb("x_norm", [P, RT, D])
        xt_hi = c.sb("xt_hi", [P, 2, KC, TB], F32R)
        xt_lo = c.sb("xt_lo", [P, 2, KC, TB], F32R)
        stats = c.sb("stats", [P, RT, 6])
        mv = c.sb("mv", [P, RT, 2])
        var_eps = c.sb("var_eps", [P, RT])
        rstd = c.sb("rstd", [P, RT])
        out_rows = c.sb("out_rows", [P, RING, D])
        out_hi = c.sb("out_hi", [P, RING, TB], F32R)
        out_lo = c.sb("out_lo", [P, RING, TB], F32R)
        turned = [c.bank(f"turned{i}") for i in range(2)]
        acc = [c.bank(f"acc{i}") for i in range(RING)]
        beta_ps = c.bank("beta_ps")
        w_rounded, w_split, beta_done, bias_kept = (
            c.sem(x) for x in ("w_rounded", "w_split", "beta_done", "bias_kept"))
        w_loaded = [c.sem(f"w_loaded{i}") for i in range(2)]
        x_loaded, stats_done, aggregated, eps_done, rstd_done, norm_done = (
            c.sem(x) for x in ("x_loaded", "stats_done", "aggregated", "eps_done", "rstd_done", "norm_done"))
        turned_done, hi_done, lo_done = (c.sem(x) for x in ("turned_done", "hi_done", "lo_done"))
        acc_done = c.sem("acc_done")
        passed = c.sem("passed")
        rows_ready, hi_ready, lo_ready = c.sem("rows_ready"), c.sem("hi_ready"), c.sem("lo_ready")
        rows_stored = [c.sem(f"rows_stored{i}") for i in range(RING)]
        cols_stored = [c.sem(f"cols_stored{i}") for i in range(RING)]

        with nc.Block() as block:
            @block.sync
            def _(sp):
                sp.dma_start(x_in[:, :, :], rows[0, :, :, :]).then_inc(x_loaded, 16)
                for n, w in enumerate(weights):
                    if n >= 2:
                        sp.wait_ge(w_split, n - 1)
                        sp.wait_ge(beta_done, n - 1)
                    sp.dma_start(w_raw[:, n % 2], w.src).then_inc(w_loaded[n % 2], 16)
                    if n == min(1, NW - 1):
                        sp.wait_ge(norm_done, RT)
                        sp.dma_start(x_in[:, :, :], rows[1, :, :, :]).then_inc(x_loaded, 16)

                def body(i, half):
                    for r in range(NR):
                        _, n, rt = groups[r]
                        sp.wait_ge(rows_ready, NR * i + r + 1)
                        sp.dma_start(row_weights[n][1][i, :, rt, :], out_rows[:, r % RING, :]).then_inc(rows_stored[r % RING], 16)
                    if not isinstance(i, int) or i + 2 < nblocks:
                        sp.wait_ge(norm_done, RT * (i + 1) + RT)
                        sp.dma_start(x_in[:, :, :], rows[i + 2, :, :, :]).then_inc(x_loaded, 16)
                    for k in range(NM):
                        _, n, m = groups[NR + k]
                        sp.wait_ge(lo_ready, NM * i + k + 1)
                        sp.dma_start(col_weights[n][1][:, m, i, :], out_hi[:, k % RING, :].bitcast(F32)).then_inc(cols_stored[k % RING], 16)
                        sp.dma_start(col_weights[n][2][:, m, i, :], out_lo[:, k % RING, :].bitcast(F32)).then_inc(cols_stored[k % RING], 16)
                each_block(sp, body)
                for slot in range(RING):
                    if NR:
                        sp.wait_ge(rows_stored[slot], 16 * (NR // RING) * nblocks)
                    sp.wait_ge(cols_stored[slot], 32 * (NM // RING) * nblocks)

            @block.gpsimd
            def _(pool):
                c.clear_last(pool)

                def body(i):
                    wait(pool, norm_done, RT * i)
                    wait_apart(pool, aggregated, RT * i + RT, passed)
                    pool.tensor_scalar(var_eps[:, :], mv[:, :, 1], EPS, None, ALU.add).then_inc(eps_done, 1)
                    pool.wait_ge(eps_done, i + 1)
                    pool.tensor_tensor(rstd[:, :], var_eps[:, :], K.halfpow[:, :], ALU.pow).then_inc(rstd_done, 1)
                each(pool, nblocks, body)

            @block.vector
            def _(dve):
                def split_weight(n, w):
                    dve.wait_ge(w_loaded[n % 2], 16 * (n // 2) + 16)
                    for kc in range(KC):
                        gain = K.col(w.gain, kc)
                        dve.tensor_scalar(w_hi[n][:, kc, :], w_raw[:, n % 2, kc, :], gain, None,
                                          ALU.mult).then_inc(w_rounded, 1)
                    for kc in range(KC):
                        gain = K.col(w.gain, kc)
                        dve.wait_ge(w_rounded, KC * n + kc + 1)
                        ins = dve.scalar_tensor_tensor(out=w_lo[n][:, kc, :], in0=w_raw[:, n % 2, kc, :], scalar=gain,
                                                       in1=w_hi[n][:, kc, :].bitcast(F32), op0=ALU.mult, op1=ALU.subtract)
                    ins.then_inc(w_split, 1)

                def keep_bias(n, w):
                    dve.wait_ge(beta_done, NW)
                    kept = K.bias[:, w.biascol:w.biascol + KC]
                    if w.extra is None:
                        dve.tensor_copy(kept, beta_ps[:, KC * n:KC * n + KC]).then_inc(bias_kept, 1)
                    else:
                        dve.tensor_tensor(kept, beta_ps[:, KC * n:KC * n + KC],
                                          K.col(w.extra, 0, KC), ALU.add).then_inc(bias_kept, 1)

                def norm(i):
                    dve.wait_ge(x_loaded, 16 * i + 16)
                    for rt in range(RT):
                        dve.bn_stats(stats[:, rt, :], x_in[:, rt, :]).then_inc(stats_done, 1)
                    for rt in range(RT):
                        wait_apart(dve, stats_done, RT * i + rt + 1, passed)
                        dve.bn_aggr(mv[:, rt, :], stats[:, rt, :]).then_inc(aggregated, 1)
                    dve.wait_ge(rstd_done, i + 1)
                    wait(dve, turned_done, KC * i)
                    for rt in range(RT):
                        dve.tensor_scalar(x_norm[:, rt, :], x_in[:, rt, :], mv[:, rt, 0:1], rstd[:, rt:rt + 1],
                                          ALU.subtract, ALU.mult).then_inc(norm_done, 1)
                norm(0)
                split_weight(0, weights[0])

                def low_parts(i, half):
                    for kc in range(KC):
                        dve.wait_ge(hi_done, KC * i + kc + 1)
                        dve.tensor_tensor(xt_lo[:, half, kc, :], turned[kc % 2][:, :], xt_hi[:, half, kc, :].bitcast(F32),
                                          ALU.subtract).then_inc(lo_done, 1)
                low_parts(0, 0)
                for n in range(1, NW):
                    split_weight(n, weights[n])
                for n, w in enumerate(weights):
                    keep_bias(n, w)
                dve.wait_ge(bias_kept, NW)

                def body(i, half):
                    if not is_last(i, nblocks):
                        norm(i + 1)
                    for k in range(NM):
                        if k == TURN_AT - NR and not is_last(i, nblocks):
                            low_parts(i + 1, 1 - half)
                        _, n, m = groups[NR + k]
                        dve.wait_ge(hi_ready, NM * i + k + 1)
                        wait(dve, cols_stored[k % RING], 32 * (NM // RING * i + k // RING))
                        dve.scalar_tensor_tensor(out=out_lo[:, k % RING, :], in0=acc[(NR + k) % RING][:, :],
                                                 scalar=K.bias_of(col_weights[n][0], m),
                                                 in1=out_hi[:, k % RING, :].bitcast(F32), op0=ALU.add,
                                                 op1=ALU.subtract).then_inc(lo_ready, 1)
                each_block(dve, body)

            @block.scalar
            def _(act):
                def high_parts(i, half):
                    for kc in range(KC):
                        act.wait_ge(turned_done, KC * i + kc + 1)
                        if kc == 0:
                            wait(act, acc_done, NG * (i - 1))
                        act.activation(xt_hi[:, half, kc, :], turned[kc % 2][:, :], ACT.Copy).then_inc(hi_done, 1)
                high_parts(0, 0)

                def body(i, half):
                    for r in range(NR):
                        act.wait_ge(acc_done, NG * i + r + 1)
                        wait(act, rows_stored[r % RING], 16 * (NR // RING * i + r // RING))
                        act.activation(out_rows[:, r % RING, :], acc[r % RING][:, :], ACT.Copy).then_inc(rows_ready, 1)
                    for k in range(NM):
                        _, n, m = groups[NR + k]
                        if k == TURN_AT - NR and not is_last(i, nblocks):
                            high_parts(i + 1, 1 - half)
                        if k == 0 and isinstance(i, int) and i == 0:
                            act.wait_ge(bias_kept, NW)
                        act.wait_ge(acc_done, NG * i + NR + k + 1)
                        wait(act, cols_stored[k % RING], 32 * (NM // RING * i + k // RING))
                        act.activation(out_hi[:, k % RING, :], acc[(NR + k) % RING][:, :], ACT.Identity,
                                       bias=K.bias_of(col_weights[n][0], m)).then_inc(hi_ready, 1)
                each_block(act, body)

            @block.tensor
            def _(pe):
                def multiply_beta(n, w):
                    pe.wait_ge(w_loaded[n % 2], 16 * (n // 2) + 16)
                    for m in range(KC):
                        for kc in range(KC):
                            ins = pe.matmul(beta_ps[:, KC * n + m:KC * n + m + 1], w_raw[:, n % 2, kc, m * P:(m + 1) * P],
                                            K.col(w.beta, kc), start=(kc == 0), stop=(kc == KC - 1))
                    ins.then_inc(beta_done, 1)

                def turn(i):
                    pe.wait_ge(norm_done, RT * i + RT)
                    for kc in range(KC):
                        if kc >= 2:
                            pe.wait_ge(lo_done, KC * i + kc - 1)
                        else:
                            wait(pe, lo_done, KC * i + kc - 1)
                        for rt in range(RT):
                            ins = pe.transpose(turned[kc % 2][:, rt * P:(rt + 1) * P], x_norm[:, rt, kc * P:(kc + 1) * P],
                                               K.ident[:, :])
                        ins.then_inc(turned_done, 1)
                turn(0)

                def body(i, half):
                    pe.wait_ge(lo_done, KC * i + KC)
                    for g, (kind, n, m) in enumerate(groups):
                        if isinstance(i, int) and i == 0 and m == 0:
                            here = n if kind == "rows" else n + len(row_weights)
                            if here < len(row_weights):
                                multiply_beta(here, weights[here])
                            elif here == len(row_weights):
                                for later in range(here, NW):
                                    multiply_beta(later, weights[later])
                            pe.wait_ge(w_split, here + 1)
                        if g == TURN_AT and not is_last(i, nblocks):
                            turn(i + 1)
                        if g >= RING:
                            back = g - RING
                            if back < NR:
                                pe.wait_ge(rows_ready, NR * i + back + 1)
                            else:
                                pe.wait_ge(lo_ready, NM * i + back - NR + 1)
                        else:
                            wait(pe, lo_ready, NM * i + g - RING + 1)
                        step = 0
                        for kc in range(KC):
                            if kind == "rows":
                                parts = split3((xt_hi[:, half, kc, m * P:(m + 1) * P], xt_lo[:, half, kc, m * P:(m + 1) * P]),
                                               (w_hi[n][:, kc, :], w_lo[n][:, kc, :]))
                            else:
                                nn = len(row_weights) + n
                                parts = split3((w_hi[nn][:, kc, m * P:(m + 1) * P], w_lo[nn][:, kc, m * P:(m + 1) * P]),
                                               (xt_hi[:, half, kc, :], xt_lo[:, half, kc, :]))
                            for lhsT, rhs in parts:
                                ins = pe.matmul(acc[g % RING][:, :], lhsT, rhs, start=(step == 0), stop=(step == 3 * KC - 1))
                                step += 1
                        ins.then_inc(acc_done, 1)
                each_block(pe, body)


class Layer:

    def __init__(self, heads, hd, stacks, max_rows, bufs, pe_units):
        self.heads, self.hd, self.stacks, self.max_rows, self.bufs = heads, hd, stacks, max_rows, bufs
        self.pe_units = pe_units
        self.nh = P // hd
        self.scale = hd ** -0.5


LAYER0 = Layer(H0, HD0, [(97, [(0, "hi"), (32, "lo"), (64, "hi")], [(0, "hi"), (32, "hi"), (64, "lo")], 96)], 96, 4, (4, 8, 13, 14))
LAYER1 = Layer(H1, HD1, [(128, [(0, "hi"), (64, "hi")], [(0, "hi"), (64, "lo")], None),
                         (96, [(0, "lo")], [(0, "hi")], 64)], 128, 4, ())


def attention(nc, phase, K, layer, k, q, v, out, qblocks, v_bias):
    NH, HD, QPS, NBUF = layer.nh, layer.hd, len(qblocks), layer.bufs
    BODY = B * QPS
    NM = NH * RT * KB
    RING = 3
    SHIFT = 3 - NM % RING
    R = NM + SHIFT
    S_UNIT = 3
    CHUNKS = 4
    FINISH = range(S_UNIT + 2, S_UNIT + CHUNKS + 4)
    SHIFT_UNIT = KT - 2
    share = [4 if u in FINISH else 5 for u in range(SHIFT_UNIT)] + [0, 0]
    m_upto = [NM * sum(share[:u]) // sum(share) for u in range(KT + 1)]
    NBLK = KC * BODY
    NLOAD = sum(len(kp) + len(qp) for _, kp, qp, _ in layer.stacks)
    QC = QPS * TB
    parts = {"hi": 0, "lo": 1}
    WIDTH = NH * TB
    POOLED = [u for u in range(KT) if u not in layer.pe_units]
    NA = len(POOLED) - 1

    with Ctx(nc, phase) as c:
        k_st = [c.sb(f"k_stack{n}", [rows, B, NH, NK], F32R) for n, (rows, *_) in enumerate(layer.stacks)]
        q_st = [c.sb(f"q_stack{n}", [rows, B, NH, QC], F32R) for n, (rows, *_) in enumerate(layer.stacks)]
        v_sb = c.sb("v", [P, B, KT, P])
        probs = c.sb("probs", [P, NBUF, WIDTH])
        sums = c.sb("sums", [P, 2, WIDTH])
        maxima = c.sb("maxima", [P, NH * RT, KB])
        top = c.sb("top", [P, NH * RT])
        top_row = c.sb("top_row", [NH * RT, P], F32R)
        sums_kept = c.sb("sums_kept", [P, TB])
        outs_kept = c.sb("outs_kept", [P, TB])
        recip = c.sb("recip", [P, TB])
        normed = c.sb("normed", [P, TB])
        out_hi = c.sb("out_hi", [P, 2, TB], F32R)
        out_lo = c.sb("out_lo", [P, 2, TB], F32R)
        work = c.bank("work", 3 + RING)
        scores = [work[:, TB * i:TB * (i + 1)] for i in (0, 1, 2, 1)]
        small = [work[:, TB * i:TB * (i + 1)] for i in range(3, 3 + RING)]
        outs, sum_ps = c.bank("outs"), c.bank("sum_ps")
        passed = c.sem("passed")
        cleared, ready = c.sem("cleared"), c.sem("ready")
        first_full, first_free = c.sem("first_full"), c.sem("first_free")
        set_loaded = [c.sem(f"set_loaded{b}") for b in range(B)]
        v_loaded = [c.sem(f"v_loaded{b}") for b in range(B)]
        scores_ready, probs_ready, pv_done = c.sem("scores_ready"), c.sem("probs_ready"), c.sem("pv_done")
        pooled, sums_done = c.sem("pooled"), c.sem("sums_done")
        small_full, small_free = c.sem("small_full"), c.sem("small_free")
        top_done, shift_loaded = c.sem("top_done"), c.sem("shift_loaded")
        outs_read, sums_read, recip_done = c.sem("outs_read"), c.sem("sums_read"), c.sem("recip_done")
        out_normed, out_rounded, out_ready = c.sem("out_normed"), c.sem("out_rounded"), c.sem("out_ready")
        out_stored = [c.sem(f"out_stored{i}") for i in range(2)]

        def place(j):
            return j // QPS % B, j % QPS

        pairs = work[:, :].rearrange("p (b t) -> p b t", t=TB)

        def use(n, x):
            return SHIFT + n * R + x, (SHIFT + x) % RING

        def uses(n):
            if is_last(n, NBLK):
                return []
            found = [(u, "max", m) for u in range(SHIFT_UNIT) for m in range(m_upto[u], m_upto[u + 1])]
            return found + [(SHIFT_UNIT, "shift", 0)]

        def pooled_upto(n, u):
            n, u = (n, u) if u >= 0 else (n - 1, u + KT)
            return NA * n + max(1, POOLED.index(u)) if u in POOLED else None

        def before(g, j):
            return (g, j - 1) if j > 0 else (g - 1, BODY - 1)

        def after(g, j):
            return (g, j + 1) if j < BODY - 1 else (g + 1, 0)

        with nc.Block() as block:
            @block.sync
            def _(sp):
                def load(g, b):
                    for n, (rows, kp, qp, _) in enumerate(layer.stacks):
                        for first, part in kp:
                            src = k[parts[part]][:, g, b * KB:(b + 1) * KB, :].rearrange("(h p) n t -> p h (n t)", p=HD)
                            sp.dma_start(k_st[n][first:first + HD, b].bitcast(F32), src).then_inc(set_loaded[b], 16)
                        for first, part in qp:
                            q0 = b * QB + qblocks[0]
                            src = q[parts[part]][:, g, q0:q0 + QPS, :].rearrange("(h p) n t -> p h (n t)", p=HD)
                            sp.dma_start(q_st[n][first:first + HD, b].bitcast(F32), src).then_inc(set_loaded[b], 16)
                    for n in range(KB):
                        src = v[b * KB + n, :, :, :].rearrange("p t (g d) -> g p t d", g=KC)[g, :, :, :]
                        sp.dma_start(v_sb[:, b, n * RT:(n + 1) * RT, :], src).then_inc(v_loaded[b], 16)

                def shift(j, at):
                    b, qb = place(j)
                    sp.wait_ge(small_free, at + SHIFT)
                    dst = q_st[-1][layer.stacks[-1][3]:layer.stacks[-1][3] + 1, b, :, qb * TB:(qb + 1) * TB]
                    for h in range(NH):
                        sp.dma_start(dst[:, h, :].bitcast(F32).rearrange("o (t c) -> o t c", t=RT),
                                     top_row[h * RT:(h + 1) * RT, :].bitcast(F32)).then_inc(shift_loaded, 16)

                def store(n, j, g):
                    b, qb = place(j)
                    wait_apart(sp, out_ready, n + 1, passed)
                    for part, src in ((0, out_hi), (1, out_lo)):
                        sp.dma_start(out[part][:, g, b * QB + qblocks[qb], :],
                                     src[:, j % 2, :].bitcast(F32)).then_inc(out_stored[j % 2], 16)

                for b in range(B):
                    load(0, b)
                sp.wait_ge(ready, 1)
                shift(0, 0)

                def body(g):
                    for j in range(BODY):
                        n = g * BODY + j
                        b, qb = place(j)
                        first = isinstance(g, int) and g == 0
                        if qb == 0 and b == 0 and not first:
                            sp.wait_ge(pv_done, KT * n)
                            load(g, B - 1)
                        if qb == 0 and b > 0 and not is_last(g, KC):
                            sp.wait_ge(pv_done, KT * n)
                            load(g + 1, b - 1)
                        if j > 0:
                            store(n - 1, j - 1, g)
                        elif not first:
                            store(n - 1, BODY - 1, g - 1)
                        if not is_last(n, NBLK):
                            at = use(n, NM)[0]
                            shift((j + 1) % BODY, at)
                each(sp, KC, body)
                store(NBLK - 1, BODY - 1, KC - 1)
                for i in range(2):
                    sp.wait_ge(out_stored[i], 32 * (NBLK // 2))

            @block.scalar
            def _(act):
                def keep_outs(n):
                    act.wait_ge(pv_done, KT * (n + 1))
                    wait(act, out_normed, n)
                    act.activation(outs_kept[:, :], outs[:, :], ACT.Copy).then_inc(outs_read, 1)

                def keep_sums(n):
                    act.wait_ge(sums_done, n + 1)
                    wait(act, recip_done, CHUNKS * n)
                    act.activation(sums_kept[:, :], sum_ps[:, :], ACT.Copy).then_inc(sums_read, 1)

                def body(g):
                    for j in range(BODY):
                        n = g * BODY + j
                        for u in range(KT):
                            U = KT * n + u
                            if not (isinstance(n, int) and n == 0):
                                if u == 1:
                                    keep_outs(n - 1)
                                elif u == S_UNIT + 1:
                                    keep_sums(n - 1)
                            for h in range(NH):
                                act.wait_ge(scores_ready, NH * U + h + 1)
                                if h == 0:
                                    wait(act, pv_done, U - NBUF + 1)
                                    added = pooled_upto(n, u - NBUF)
                                    if added is not None:
                                        wait(act, pooled, added)
                                act.activation(probs[:, (KT * j + u) % NBUF, h * TB:(h + 1) * TB],
                                               scores[(NH * u + h) % 4], ACT.Exp, scale=layer.scale).then_inc(probs_ready, 1)

                each(act, KC, body)
                keep_outs(NBLK - 1)
                keep_sums(NBLK - 1)

            @block.gpsimd
            def _(pool):
                c.clear_last(pool)
                rows, shift_row = layer.stacks[-1][0], layer.stacks[-1][3]
                if rows > shift_row + 1:
                    pool.memset(k_st[-1][shift_row:rows].bitcast(F32), 0.0)
                    pool.memset(q_st[-1][shift_row:rows].bitcast(F32), 0.0).then_inc(cleared, 1)
                    pool.wait_ge(cleared, 1)
                pool.memset(k_st[-1][shift_row:shift_row + 1].bitcast(F32), -1.0).then_inc(ready, 1)

                def body(g):
                    for j in range(BODY):
                        n = g * BODY + j
                        acc = sums[:, j % 2, :]
                        for i in range(1, NA + 1):
                            u = POOLED[i]
                            pool.wait_ge(probs_ready, NH * (KT * n + u + 1))
                            if i == 1:
                                wait(pool, sums_done, n - 1)
                                old = probs[:, (KT * j + POOLED[0]) % NBUF, :]
                            else:
                                pool.wait_ge(pooled, NA * n + i - 1)
                                old = acc
                            pool.tensor_tensor(acc, old, probs[:, (KT * j + u) % NBUF, :], ALU.add).then_inc(pooled, 1)
                each(pool, KC, body)

            @block.vector
            def _(dve):
                def take_max(m, at, slot):
                    dve.wait_ge(small_full, at + 1)
                    dve.tensor_reduce(maxima[:, m // KB, m % KB:m % KB + 1], small[slot], AX.X,
                                      ALU.max).then_inc(small_free, 1)

                def take_shift(n, at, slot):
                    dve.wait_ge(small_full, at + SHIFT)
                    wait(dve, shift_loaded, 16 * NH * n)
                    dve.tensor_copy(top_row[:, :], small[slot][0:NH * RT, 0:P]).then_inc(small_free, SHIFT)

                def take_top(at):
                    dve.wait_ge(small_free, at)
                    dve.tensor_reduce(top[:, :], maxima[:, :, :], AX.X, ALU.max).then_inc(top_done, 1)

                def finish(g, j, step):
                    n, jj = g * BODY + j, j % 2
                    bias = v_bias[:, bass.ds(g, 1)]
                    if step < CHUNKS:
                        cols = slice(step * TB // CHUNKS, (step + 1) * TB // CHUNKS)
                        if step == 0:
                            dve.wait_ge(sums_read, n + 1)
                            wait(dve, out_normed, n)
                        dve.reciprocal(recip[:, cols], sums_kept[:, cols]).then_inc(recip_done, 1)
                    elif step == CHUNKS:
                        dve.wait_ge(recip_done, CHUNKS * (n + 1))
                        dve.wait_ge(outs_read, n + 1)
                        dve.tensor_tensor(normed[:, :], outs_kept[:, :], recip[:, :], ALU.mult).then_inc(out_normed, 1)
                        dve.wait_ge(out_normed, n + 1)
                        wait(dve, out_stored[jj], 32 * (g * (BODY // 2) + j // 2))
                        dve.tensor_scalar(out_hi[:, jj, :], normed[:, :], bias, None, ALU.add).then_inc(out_rounded, 1)
                    else:
                        dve.wait_ge(out_rounded, n + 1)
                        dve.scalar_tensor_tensor(out=out_lo[:, jj, :], in0=normed[:, :], scalar=bias,
                                                 in1=out_hi[:, jj, :].bitcast(F32), op0=ALU.add,
                                                 op1=ALU.subtract).then_inc(out_ready, 1)

                for i in range(NM // 2):
                    dve.wait_ge(first_full, i + 1)
                    dve.tensor_reduce(maxima[:, 2 * i // KB, 2 * i % KB:2 * i % KB + 2],
                                      pairs[:, 2 * (i % 3):2 * (i % 3) + 2, :], AX.X,
                                      ALU.max).then_inc(first_free, 1)
                dve.wait_ge(first_free, NM // 2)
                dve.tensor_reduce(top[:, :], maxima[:, :, :], AX.X, ALU.max).then_inc(top_done, 1)
                take_shift(0, 0, 0)

                def body(g):
                    for j in range(BODY):
                        n = g * BODY + j
                        for u in range(KT):
                            mine = [(x, kind, m) for x, (unit, kind, m) in enumerate(uses(n)) if unit == u]
                            for i, (x, kind, m) in enumerate(mine):
                                if i < NH:
                                    take(n, x, kind, m)
                            if u in FINISH and not (isinstance(n, int) and n == 0):
                                finish(*before(g, j), u - FINISH[0])
                            for x, kind, m in mine[NH:]:
                                take(n, x, kind, m)
                            if u == SHIFT_UNIT - 1 and not is_last(n, NBLK):
                                take_top(use(n, NM)[0])

                def take(n, x, kind, m):
                    if kind == "max":
                        take_max(m, *use(n, x))
                    else:
                        take_shift(n + 1, *use(n, x))
                each(dve, KC, body)
                for step in range(len(FINISH)):
                    finish(KC - 1, BODY - 1, step)

            @block.tensor
            def _(pe):
                def product_for_max(g, j, m, bank):
                    b, qb = place(j)
                    h, qt, kb = m // KB // RT, m // KB % RT, m % KB
                    if m == 0 and qb == 0:
                        pe.wait_ge(set_loaded[b], 16 * NLOAD * (g + 1))
                    rows = layer.max_rows
                    q0 = qb * TB + qt * P
                    return pe.matmul(bank, q_st[0][0:rows, b, h, q0:q0 + P],
                                     k_st[0][0:rows, b, h, kb * TB:(kb + 1) * TB], start=True, stop=True)

                def next_max(n, g, j, x, m):
                    at, slot = use(n, x)
                    wait(pe, small_free, at - RING + 1)
                    product_for_max(*after(g, j), m, small[slot]).then_inc(small_full, 1)

                def turn_shift(n, at, slot):
                    pe.wait_ge(top_done, n + 1)
                    wait(pe, small_free, at - RING + 1)
                    pe.transpose(small[slot][0:NH * RT, 0:P], top[:, :], K.ident[:, :]).then_inc(small_full, SHIFT)

                def multiply_v(g, j, kt):
                    n, (b, qb) = g * BODY + j, place(j)
                    U = KT * n + kt
                    pe.wait_ge(probs_ready, NH * (U + 1))
                    if kt == 0 and qb == 0:
                        pe.wait_ge(v_loaded[b], 16 * KB * (g + 1))
                    if kt == 0:
                        wait(pe, outs_read, n)
                    new = probs[:, (KT * j + kt) % NBUF, :]
                    for h in range(NH):
                        ins = pe.matmul(outs[h * HD:(h + 1) * HD, :], v_sb[:, b, kt, h * HD:(h + 1) * HD],
                                        new[:, h * TB:(h + 1) * TB], start=(kt == 0), stop=(kt == KT - 1))
                    if kt in layer.pe_units:
                        first = kt == layer.pe_units[0]
                        if first:
                            wait(pe, sums_read, n)
                        for h in range(NH):
                            ins = pe.matmul(sum_ps[h * HD:(h + 1) * HD, :], K.ones[:, 0:HD], new[:, h * TB:(h + 1) * TB],
                                            start=first, stop=False)
                    ins.then_inc(pv_done, 1)

                def multiply_sums(g, j):
                    n = g * BODY + j
                    pe.wait_ge(pooled, NA * (n + 1))
                    if not layer.pe_units:
                        wait(pe, sums_read, n)
                    for h in range(NH):
                        ins = pe.matmul(sum_ps[h * HD:(h + 1) * HD, :], K.ones[:, 0:HD],
                                        sums[:, j % 2, h * TB:(h + 1) * TB], start=not layer.pe_units, stop=True)
                    ins.then_inc(sums_done, 1)

                pe.wait_ge(ready, 1)
                for m in range(NM):
                    i = m // 2
                    if m % 2 == 0 and i >= 3:
                        pe.wait_ge(first_free, i - 2)
                    ins = product_for_max(0, 0, m, pairs[:, 2 * (i % 3) + m % 2, :])
                    if m % 2:
                        ins.then_inc(first_full, 1)
                turn_shift(0, 0, 0)

                def body(g):
                    for j in range(BODY):
                        n = g * BODY + j
                        b, qb = place(j)
                        for u in range(KT):
                            U = KT * n + u
                            mine = [(x, kind, m) for x, (unit, kind, m) in enumerate(uses(n)) if unit == u]
                            maxes = [(x, m) for x, kind, m in mine if kind == "max"]
                            shifts = [x for x, kind, _ in mine if kind == "shift"]
                            for x in shifts:
                                turn_shift(n + 1, *use(n, x))
                            for h in range(NH):
                                for x, m in maxes[h:h + 1]:
                                    next_max(n, g, j, x, m)
                                X = NH * U + h
                                wait(pe, probs_ready, X - 1 if h % 2 else X - 3)
                                if u == 0 and h == 0:
                                    pe.wait_ge(shift_loaded, 16 * NH * (n + 1))
                                for s, (rows, *_) in enumerate(layer.stacks):
                                    ins = pe.matmul(scores[(NH * u + h) % 4], k_st[s][0:rows, b, h, u * P:(u + 1) * P],
                                                    q_st[s][0:rows, b, h, qb * TB:(qb + 1) * TB],
                                                    start=(s == 0), stop=(s == len(layer.stacks) - 1))
                                ins.then_inc(scores_ready, 1)
                            for x, m in maxes[NH:]:
                                next_max(n, g, j, x, m)
                            if u > 0:
                                multiply_v(g, j, u - 1)
                            elif not (isinstance(n, int) and n == 0):
                                multiply_v(*before(g, j), KT - 1)
                            if u == S_UNIT and not (isinstance(n, int) and n == 0):
                                multiply_sums(*before(g, j))
                each(pe, KC, body)
                multiply_v(KC - 1, BODY - 1, KT - 1)
                multiply_sums(KC - 1, BODY - 1)


def project_and_add(nc, phase, K, w_src, a, residual, bias, out):
    NB = B * QB
    RING = 4
    with Ctx(nc, phase) as c:
        w_raw = c.sb("w_raw", [P, KC, D])
        w = (c.sb("w_hi", [P, KC, D], F32R), c.sb("w_lo", [P, KC, D], F32R))
        a_sb = [c.sb(f"a_{x}", [P, 2, KC, TB], F32R) for x in ("hi", "lo")]
        res = c.sb("res", [P, 2, KC, TB])
        res_b = c.sb("res_b", [P, 2, KC, TB])
        y = c.sb("y", [P, RING, TB])
        acc = [c.bank(f"acc{i}") for i in range(RING)]
        w_loaded, w_rounded, w_split = c.sem("w_loaded"), c.sem("w_rounded"), c.sem("w_split")
        loaded = [c.sem(f"loaded{i}") for i in range(2)]
        acc_done, biased, y_ready = c.sem("acc_done"), c.sem("biased"), c.sem("y_ready")
        stored = [c.sem(f"stored{i}") for i in range(RING)]
        with nc.Block() as block:
            @block.sync
            def _(sp):
                sp.dma_start(w_raw[:, :, :], w_src).then_inc(w_loaded, 16)

                def load(i):
                    for part in range(2):
                        sp.dma_start(a_sb[part][:, i % 2].bitcast(F32), a[part][:, :, i, :]).then_inc(loaded[i % 2], 16)
                    sp.dma_start(res[:, i % 2], residual[:, :, i, :]).then_inc(loaded[i % 2], 16)
                load(0)
                load(1)
                for i in range(NB):
                    for m in range(KC):
                        sp.wait_ge(y_ready, KC * i + m + 1)
                        sp.dma_start(out[:, m, i, :], y[:, m, :]).then_inc(stored[m], 16)
                    if i + 2 < NB:
                        load(i + 2)
                for m in range(KC):
                    sp.wait_ge(stored[m], 16 * NB)

            @block.gpsimd
            def _(pool):
                c.clear_last(pool)

            @block.vector
            def _(dve):
                dve.wait_ge(w_loaded, 16)
                for kc in range(KC):
                    dve.tensor_copy(w[0][:, kc, :], w_raw[:, kc, :]).then_inc(w_rounded, 1)
                for kc in range(KC):
                    dve.wait_ge(w_rounded, kc + 1)
                    dve.tensor_tensor(w[1][:, kc, :], w_raw[:, kc, :], w[0][:, kc, :].bitcast(F32),
                                      ALU.subtract).then_inc(w_split, 1)
                for i in range(NB):
                    dve.wait_ge(loaded[i % 2], 48 * (i // 2 + 1))
                    for m in range(KC):
                        dve.tensor_scalar(res_b[:, i % 2, m, :], res[:, i % 2, m, :], bias[:, m:m + 1], None,
                                          ALU.add).then_inc(biased, 1)
                    for m in range(KC):
                        dve.wait_ge(biased, KC * i + m + 1)
                        dve.wait_ge(acc_done, KC * i + m + 1)
                        if i:
                            dve.wait_ge(stored[m], 16 * i)
                        dve.tensor_tensor(y[:, m, :], res_b[:, i % 2, m, :], acc[m][:, :], ALU.add).then_inc(y_ready, 1)

            @block.tensor
            def _(pe):
                pe.wait_ge(w_split, KC)
                for i in range(NB):
                    pe.wait_ge(loaded[i % 2], 48 * (i // 2 + 1))
                    for m in range(KC):
                        if i:
                            pe.wait_ge(y_ready, KC * (i - 1) + m + 1)
                        step = 0
                        for kc in range(KC):
                            for lhsT, rhs in split3((w[0][:, kc, m * P:(m + 1) * P], w[1][:, kc, m * P:(m + 1) * P]),
                                                    (a_sb[0][:, i % 2, kc, :], a_sb[1][:, i % 2, kc, :])):
                                ins = pe.matmul(acc[m][:, :], lhsT, rhs, start=(step == 0), stop=(step == 3 * KC - 1))
                                step += 1
                        ins.then_inc(acc_done, 1)


def feed_forward(nc, phase, K, w1_src, w2_src, x, out):
    NB = B * QB
    LAG = 2
    RING = 3
    with Ctx(nc, phase) as c:
        w1 = (c.sb("w1_hi", [P, KC, DFF], F32R), c.sb("w1_lo", [P, KC, DFF], F32R))
        w2 = (c.sb("w2_hi", [P, FC, D], F32R), c.sb("w2_lo", [P, FC, D], F32R))
        x_sb = c.sb("x", [P, KC, TB])
        xs = (c.sb("x_hi", [P, KC, TB], F32R), c.sb("x_lo", [P, KC, TB], F32R))
        x_b = c.sb("x_b", [P, KC, TB])
        th = c.sb("tanh", [P, 2, TB])
        z = c.sb("z", [P, 2, TB])
        h2 = c.sb("h2", [P, 2, TB])
        hs = (c.sb("h_hi", [P, RING, TB], F32R), c.sb("h_lo", [P, RING, TB], F32R))
        y = x_b
        z_ps = [c.bank(f"z{i}") for i in range(2)]
        y_ps = [c.bank(f"y{i}") for i in range(KC)]
        w_loaded = [c.sem(f"w_loaded{i}") for i in range(2)]
        w_rounded, w_split = c.sem("w_rounded"), c.sem("w_split")
        loaded, x_rounded, x_split, biased = c.sem("loaded"), c.sem("x_rounded"), c.sem("x_split"), c.sem("biased")
        z_done, z_kept, h_done, h_rounded, h_split = (
            c.sem("z_done"), c.sem("z_kept"), c.sem("h_done"), c.sem("h_rounded"), c.sem("h_split"))
        tanh_done = c.sem("tanh_done")
        y_multiplied, y_done, y_ready, stored = c.sem("y_multiplied"), c.sem("y_done"), c.sem("y_ready"), c.sem("stored")
        raw = [buf[:, :, :, :].rearrange("p l b c -> p (l b c)")[:, 0:KC * D].rearrange("p (k d) -> p k d", d=D)
               for buf in (K.drive, K.hist)]
        PER = KC
        NPC = 2 * FC // PER

        def raw_src(q):
            return w1_src[:, :, q // 2 * D:(q // 2 + 1) * D] if q % 2 == 0 else w2_src[:, q // 2 * PER:(q // 2 + 1) * PER, :]

        def split_part(q, k, part):
            return w1[part][:, k, q // 2 * D:(q // 2 + 1) * D] if q % 2 == 0 else w2[part][:, q // 2 * PER + k, :]

        with nc.Block() as block:
            @block.sync
            def _(sp):
                for q in range(NPC):
                    if q >= 2:
                        sp.wait_ge(w_split, PER * (q - 1))
                    sp.dma_start(raw[q % 2], raw_src(q)).then_inc(w_loaded[q % 2], 16)
                    if q == 0:
                        sp.dma_start(x_sb[:, :, :], x[:, :, 0, :]).then_inc(loaded, 16)
                for i in range(NB):
                    if i + 1 < NB:
                        sp.wait_ge(x_split, KC * (i + 1))
                        sp.wait_ge(biased, KC * (i + 1))
                        sp.dma_start(x_sb[:, :, :], x[:, :, i + 1, :]).then_inc(loaded, 16)
                    sp.wait_ge(y_ready, KC * (i + 1))
                    sp.dma_start(out[:, :, i, :], y[:, :, :]).then_inc(stored, 16)
                sp.wait_ge(stored, 16 * NB)

            @block.scalar
            def _(act):
                for i in range(NB):
                    for f in range(FC):
                        n = FC * i + f
                        act.wait_ge(z_done, n + 1)
                        if n >= 2:
                            act.wait_ge(h_done, n - 1)
                        act.activation(th[:, n % 2, :], z_ps[n % 2][:, :], ACT.Tanh, bias=K.half_b1[:, f:f + 1],
                                       scale=0.5).then_inc(tanh_done, 1)
                        act.activation(z[:, n % 2, :], z_ps[n % 2][:, :], ACT.Identity,
                                       bias=K.col("b1", f)).then_inc(z_kept, 1)

            @block.gpsimd
            def _(pool):
                c.clear_last(pool)

            @block.vector
            def _(dve):
                def split_weights(q):
                    dve.wait_ge(w_loaded[q % 2], 16 * (q // 2) + 16)
                    for k in range(PER):
                        dve.tensor_copy(split_part(q, k, 0), raw[q % 2][:, k, :]).then_inc(w_rounded, 1)
                    for k in range(PER):
                        dve.wait_ge(w_rounded, PER * q + k + 1)
                        dve.tensor_tensor(split_part(q, k, 1), raw[q % 2][:, k, :], split_part(q, k, 0).bitcast(F32),
                                          ALU.subtract).then_inc(w_split, 1)
                split_weights(0)
                def split_x(i):
                    dve.wait_ge(loaded, 16 * i + 16)
                    if i:
                        dve.wait_ge(z_done, FC * i)
                    for kc in range(KC):
                        dve.tensor_copy(xs[0][:, kc, :], x_sb[:, kc, :]).then_inc(x_rounded, 1)
                    for kc in range(KC):
                        dve.wait_ge(x_rounded, KC * i + kc + 1)
                        dve.tensor_tensor(xs[1][:, kc, :], x_sb[:, kc, :], xs[0][:, kc, :].bitcast(F32),
                                          ALU.subtract).then_inc(x_split, 1)
                split_x(0)
                for i in range(NB):
                    for f in range(FC):
                        if i == 0 and f % 2 == 0 and f // 2 + 1 < NPC:
                            split_weights(f // 2 + 1)
                        if f == KC:
                            if i:
                                dve.wait_ge(stored, 16 * i)
                            for m in range(KC):
                                dve.tensor_scalar(x_b[:, m, :], x_sb[:, m, :], K.col("b2", m), None,
                                                  ALU.add).then_inc(biased, 1)
                        n = FC * i + f
                        dve.wait_ge(tanh_done, n + 1)
                        dve.wait_ge(z_kept, n + 1)
                        if n >= 2:
                            dve.wait_ge(h_split, n - 1)
                        dve.scalar_tensor_tensor(out=h2[:, n % 2, :], in0=th[:, n % 2, :], scalar=1.0, in1=z[:, n % 2, :],
                                                 op0=ALU.add, op1=ALU.mult).then_inc(h_done, 1)
                        dve.wait_ge(h_done, n + 1)
                        if n >= RING:
                            dve.wait_ge(y_multiplied, n - RING + 1)
                        dve.tensor_copy(hs[0][:, n % RING, :], h2[:, n % 2, :]).then_inc(h_rounded, 1)
                        dve.wait_ge(h_rounded, n + 1)
                        dve.tensor_tensor(hs[1][:, n % RING, :], h2[:, n % 2, :], hs[0][:, n % RING, :].bitcast(F32),
                                          ALU.subtract).then_inc(h_split, 1)
                    if i + 1 < NB:
                        split_x(i + 1)
                    dve.wait_ge(y_multiplied, FC * (i + 1))
                    dve.wait_ge(biased, KC * (i + 1))
                    for m in range(KC):
                        dve.scalar_tensor_tensor(out=y[:, m, :], in0=y_ps[m][:, :], scalar=0.5, in1=x_b[:, m, :],
                                                 op0=ALU.mult, op1=ALU.add).then_inc(y_ready, 1)

            @block.tensor
            def _(pe):
                def hidden(n):
                    f = n % FC
                    if n < FC and f % PER == 0:
                        pe.wait_ge(w_split, PER * (2 * (f // PER) + 1))
                    if n >= 2:
                        pe.wait_ge(z_kept, n - 1)
                    step = 0
                    for kc in range(KC):
                        for lhsT, rhs in split3((w1[0][:, kc, f * P:(f + 1) * P], w1[1][:, kc, f * P:(f + 1) * P]),
                                                (xs[0][:, kc, :], xs[1][:, kc, :])):
                            ins = pe.matmul(z_ps[n % 2][:, :], lhsT, rhs, start=(step == 0), stop=(step == 3 * KC - 1))
                            step += 1
                    ins.then_inc(z_done, 1)

                def down(n):
                    f = n % FC
                    if n < FC and f % PER == 0:
                        pe.wait_ge(w_split, PER * (2 * (f // PER) + 2))
                    pe.wait_ge(h_split, n + 1)
                    if f == 0 and n:
                        pe.wait_ge(y_ready, KC * (n // FC))
                    for m in range(KC):
                        for s, (lhsT, rhs) in enumerate(split3(
                                (w2[0][:, f, m * P:(m + 1) * P], w2[1][:, f, m * P:(m + 1) * P]),
                                (hs[0][:, n % RING, :], hs[1][:, n % RING, :]))):
                            ins = pe.matmul(y_ps[m][:, :], lhsT, rhs, start=(f == 0 and s == 0), stop=(f == FC - 1 and s == 2))
                    ins.then_inc(y_multiplied, 1)

                for i in range(NB):
                    pe.wait_ge(x_split, KC * (i + 1))
                    for f in range(FC + LAG):
                        if f < FC:
                            hidden(FC * i + f)
                        if f >= LAG:
                            down(FC * i + f - LAG)


SL = 16
SC = NQ // SL
SN = B * SC
ALIKE = 2.0 ** -19


def normalize_features(nc, phase, K, x, gain, beta, w_src, extra, biascol, out, recurrence=None):
    NB = B * QB
    W = P if recurrence else D
    MO = W // P
    with Ctx(nc, phase) as c:
        w_raw = c.sb("w_raw", [P, KC, W])
        w = (c.sb("w_hi", [P, KC, W], F32R), c.sb("w_lo", [P, KC, W], F32R))
        x_sb = c.sb("x", [P, 2, KC, TB])
        centred = c.sb("centred", [P, 2, KC, TB])
        squared = c.sb("squared", [P, KC, TB])
        var_eps = c.sb("var_eps", [P, TB])
        std = c.sb("std", [P, TB])
        guess = c.sb("guess", [P, 3, TB])
        rstd = c.sb("rstd", [P, TB])
        xn = c.sb("xn", [P, KC, TB])
        xs = (c.sb("x_hi", [P, KC, TB], F32R), c.sb("x_lo", [P, KC, TB], F32R))
        o_hi = c.sb("o_hi", [P, KC, TB], F32R)
        o_lo = c.sb("o_lo", [P, KC, TB], F32R)
        mean_ps, var_ps, bias_ps = c.bank("mean_ps"), c.bank("var_ps"), c.bank("bias_ps")
        acc = [c.bank(f"acc{i}") for i in range(4)]
        w_loaded, w_made, w_rounded, w_split = c.sem("w_loaded"), c.sem("w_made"), c.sem("w_rounded"), c.sem("w_split")
        bias_done, bias_kept = c.sem("bias_done"), c.sem("bias_kept")
        loaded = [c.sem(f"loaded{i}") for i in range(2)]
        mean_done, centred_done, squared_done, var_done = (
            c.sem("mean_done"), c.sem("centred_done"), c.sem("squared_done"), c.sem("var_done"))
        eps_done, std_done, guessed, rstd_done, xn_done, x_rounded, x_split = (
            c.sem("eps_done"), c.sem("std_done"), c.sem("guessed"), c.sem("rstd_done"), c.sem("xn_done"), c.sem("x_rounded"), c.sem("x_split"))
        acc_done, hi_ready, lo_ready = c.sem("acc_done"), c.sem("hi_ready"), c.sem("lo_ready")
        stored = [c.sem(f"stored{i}") for i in range(KC)]
        if recurrence:
            w_in = c.sb("w_in", [P, KC, D])
            bmat = c.sb("bmat", [P, KC, S])
            wbt = c.sb("wbt", [S, D])
            side = c.sb("side", [S, P])
            bb = c.sb("bb", [S, 1])
            prep_ps = c.bank("prep_ps")
            made, prep_done = c.sem("made"), c.sem("prep_done")
        bias = K.bias[:, biascol:biascol + MO]

        with nc.Block() as block:
            @block.sync
            def _(sp):
                if recurrence:
                    sp.dma_start(w_in[:, :, :], recurrence["w_in"].rearrange("(c p) i -> p c i", p=P)).then_inc(w_loaded, 16)
                    sp.dma_start(bmat[:, :, :], recurrence["bmat"].rearrange("(c p) s -> p c s", p=P)).then_inc(w_loaded, 16)
                    sp.dma_start(side[:, S:P], recurrence["aT"]).then_inc(w_loaded, 16)
                else:
                    sp.dma_start(w_raw[:, :, :], w_src).then_inc(w_loaded, 16)
                for i in range(NB):
                    if i >= 2:
                        sp.wait_ge(centred_done, KC * (i - 1))
                    sp.dma_start(x_sb[:, i % 2], x[:, :, i, :]).then_inc(loaded[i % 2], 16)
                if not recurrence:
                    for i in range(NB):
                        for m in range(KC):
                            sp.wait_ge(lo_ready, KC * i + m + 1)
                            sp.dma_start(out[0][:, m, i, :], o_hi[:, m, :].bitcast(F32)).then_inc(stored[m], 16)
                            sp.dma_start(out[1][:, m, i, :], o_lo[:, m, :].bitcast(F32)).then_inc(stored[m], 16)
                    for m in range(KC):
                        sp.wait_ge(stored[m], 32 * NB)

            @block.gpsimd
            def _(pool):
                c.clear_last(pool)

            @block.scalar
            def _(act):
                def square(i):
                    for kc in range(KC):
                        act.wait_ge(centred_done, KC * i + kc + 1)
                        if i and kc == 0:
                            act.wait_ge(var_done, i)
                        act.activation(squared[:, kc, :], centred[:, i % 2, kc, :], ACT.Square).then_inc(squared_done, 1)
                def root(i):
                    act.wait_ge(eps_done, i + 1)
                    act.activation(std[:, :], var_eps[:, :], ACT.Sqrt).then_inc(std_done, 1)
                square(0)
                root(0)
                square(1)
                for i in range(NB):
                    for kc in range(KC):
                        act.wait_ge(xn_done, KC * i + kc + 1)
                        if i and kc == 0:
                            act.wait_ge(acc_done, MO * i)
                        act.activation(xs[0][:, kc, :], xn[:, kc, :], ACT.Copy).then_inc(x_rounded, 1)
                    if i + 1 < NB:
                        root(i + 1)
                    if i + 2 < NB:
                        square(i + 2)
                    if i == 0:
                        act.wait_ge(bias_kept, 1)
                    for m in range(MO):
                        act.wait_ge(acc_done, MO * i + m + 1)
                        if recurrence:
                            b, run = i // QB, i % QB * (TB // SL)
                            act.activation(K.drive[:, 1:SL + 1, b, run:run + TB // SL],
                                           acc[i % 4][:, :].rearrange("p (r l) -> p l r", l=SL), ACT.Identity,
                                           bias=bias).then_inc(hi_ready, 1)
                        else:
                            if i:
                                act.wait_ge(stored[m], 32 * i)
                            act.activation(o_hi[:, m, :], acc[m][:, :], ACT.Identity,
                                           bias=bias[:, m:m + 1]).then_inc(hi_ready, 1)

            @block.vector
            def _(dve):
                if recurrence:
                    dve.tensor_copy(side[:, 0:S], K.ident[0:S, 0:S]).then_inc(made, 1)
                    dve.wait_ge(prep_done, 1)
                    dve.tensor_copy(wbt[:, :], prep_ps[0:S, :]).then_inc(made, 1)
                    dve.wait_ge(prep_done, 2)
                    dve.tensor_copy(bb[:, :], bias_ps[0:S, 0:1]).then_inc(made, 1)
                    dve.wait_ge(prep_done, 3)
                    dve.tensor_copy(w_raw[:, :, :], prep_ps[:, :]).then_inc(w_made, 1)
                    dve.wait_ge(w_made, 1)
                else:
                    dve.wait_ge(w_loaded, 16)
                for kc in range(KC):
                    dve.tensor_scalar(w[0][:, kc, :], w_raw[:, kc, :], K.col(gain, kc), None, ALU.mult).then_inc(w_rounded, 1)
                for kc in range(KC):
                    dve.wait_ge(w_rounded, kc + 1)
                    dve.scalar_tensor_tensor(out=w[1][:, kc, :], in0=w_raw[:, kc, :], scalar=K.col(gain, kc),
                                             in1=w[0][:, kc, :].bitcast(F32), op0=ALU.mult,
                                             op1=ALU.subtract).then_inc(w_split, 1)

                def centre(i):
                    dve.wait_ge(loaded[i % 2], 16 * (i // 2 + 1))
                    dve.wait_ge(mean_done, i + 1)
                    if i >= 2:
                        dve.wait_ge(xn_done, KC * (i - 1))
                        dve.wait_ge(squared_done, KC * (i - 1))
                    for kc in range(KC):
                        dve.scalar_tensor_tensor(out=centred[:, i % 2, kc, :], in0=mean_ps[:, :], scalar=-1.0 / D,
                                                 in1=x_sb[:, i % 2, kc, :], op0=ALU.mult, op1=ALU.add).then_inc(centred_done, 1)
                def rstd_of(i):
                    dve.wait_ge(var_done, i + 1)
                    dve.tensor_scalar(var_eps[:, :], var_ps[:, :], 1.0 / D, EPS, ALU.mult, ALU.add).then_inc(eps_done, 1)
                    dve.wait_ge(std_done, i + 1)
                    dve.reciprocal(guess[:, 0, :], std[:, :]).then_inc(guessed, 1)
                    dve.wait_ge(guessed, 3 * i + 1)
                    dve.scalar_tensor_tensor(out=guess[:, 1, :], in0=var_eps[:, :], scalar=-0.5, in1=guess[:, 0, :],
                                             op0=ALU.mult, op1=ALU.mult).then_inc(guessed, 1)
                    dve.wait_ge(guessed, 3 * i + 2)
                    dve.tensor_tensor(guess[:, 2, :], guess[:, 1, :], guess[:, 0, :], ALU.mult).then_inc(guessed, 1)
                    dve.wait_ge(guessed, 3 * i + 3)
                    dve.scalar_tensor_tensor(out=rstd[:, :], in0=guess[:, 2, :], scalar=1.5, in1=guess[:, 0, :],
                                             op0=ALU.add, op1=ALU.mult).then_inc(rstd_done, 1)
                centre(0)
                rstd_of(0)
                centre(1)
                dve.wait_ge(bias_done, 1)
                if extra is None:
                    dve.tensor_copy(bias, bias_ps[:, 8:8 + MO]).then_inc(bias_kept, 1)
                else:
                    dve.tensor_tensor(bias, bias_ps[:, 8:8 + MO], K.col(extra, 0, MO), ALU.add).then_inc(bias_kept, 1)
                dve.wait_ge(bias_kept, 1)
                for i in range(NB):
                    dve.wait_ge(rstd_done, i + 1)
                    for kc in range(KC):
                        if i:
                            dve.wait_ge(x_split, KC * (i - 1) + kc + 1)
                        dve.wait_ge(centred_done, KC * i + kc + 1)
                        dve.tensor_tensor(xn[:, kc, :], centred[:, i % 2, kc, :], rstd[:, :], ALU.mult).then_inc(xn_done, 1)
                    for kc in range(KC):
                        dve.wait_ge(x_rounded, KC * i + kc + 1)
                        dve.tensor_tensor(xs[1][:, kc, :], xn[:, kc, :], xs[0][:, kc, :].bitcast(F32),
                                          ALU.subtract).then_inc(x_split, 1)
                    if i + 1 < NB:
                        rstd_of(i + 1)
                    if i + 2 < NB:
                        centre(i + 2)
                    if not recurrence:
                        for m in range(MO):
                            dve.wait_ge(hi_ready, MO * i + m + 1)
                            if i:
                                dve.wait_ge(stored[m], 32 * i)
                            dve.scalar_tensor_tensor(out=o_lo[:, m, :], in0=acc[m][:, :], scalar=bias[:, m:m + 1],
                                                     in1=o_hi[:, m, :].bitcast(F32), op0=ALU.add,
                                                     op1=ALU.subtract).then_inc(lo_ready, 1)
                if recurrence:
                    dve.wait_ge(hi_ready, NB)
                    dve.tensor_copy(K.drive[:, 0, :, 1:SC], K.drive[:, SL, :, 0:SC - 1])
                    dve.memset(K.drive[:, 0, :, 0:1], 0.0)

            @block.tensor
            def _(pe):
                def mean(i):
                    pe.wait_ge(loaded[i % 2], 16 * (i // 2 + 1))
                    if i:
                        pe.wait_ge(centred_done, KC * i)
                    for kc in range(KC):
                        ins = pe.matmul(mean_ps[:, :], K.ones[:, :], x_sb[:, i % 2, kc, :], start=(kc == 0), stop=(kc == KC - 1))
                    ins.then_inc(mean_done, 1)

                def variance(i):
                    if i:
                        pe.wait_ge(eps_done, i)
                    for kc in range(KC):
                        pe.wait_ge(squared_done, KC * i + kc + 1)
                        ins = pe.matmul(var_ps[:, :], K.ones[:, :], squared[:, kc, :], start=(kc == 0), stop=(kc == KC - 1))
                    ins.then_inc(var_done, 1)

                if recurrence:
                    pe.wait_ge(w_loaded, 48)
                    for oc in range(KC):
                        ins = pe.matmul(prep_ps[0:S, :], bmat[:, oc, :], w_in[:, oc, :], start=(oc == 0), stop=(oc == KC - 1))
                    ins.then_inc(prep_done, 1)
                    for oc in range(KC):
                        ins = pe.matmul(bias_ps[0:S, 0:1], bmat[:, oc, :], K.col("b_in", oc), start=(oc == 0), stop=(oc == KC - 1))
                    ins.then_inc(prep_done, 1)
                    pe.wait_ge(made, 3)
                    for kc in range(KC):
                        ins = pe.matmul(prep_ps[:, kc * P:(kc + 1) * P], wbt[:, kc * P:(kc + 1) * P], side[:, :],
                                        start=True, stop=True)
                    ins.then_inc(prep_done, 1)
                    pe.wait_ge(w_made, 1)
                    for kc in range(KC):
                        pe.matmul(bias_ps[:, 8:9], w_raw[:, kc, :], K.col(beta, kc), start=(kc == 0), stop=False)
                    pe.matmul(bias_ps[:, 8:9], side[:, :], bb[:, :], start=False, stop=True).then_inc(bias_done, 1)
                else:
                    pe.wait_ge(w_loaded, 16)
                    for m in range(MO):
                        for kc in range(KC):
                            ins = pe.matmul(bias_ps[:, 8 + m:9 + m], w_raw[:, kc, m * P:(m + 1) * P], K.col(beta, kc),
                                            start=(kc == 0), stop=(kc == KC - 1))
                    ins.then_inc(bias_done, 1)
                mean(0)
                variance(0)
                mean(1)
                variance(1)
                pe.wait_ge(w_split, KC)
                for i in range(NB):
                    if i + 2 < NB:
                        mean(i + 2)
                    pe.wait_ge(x_split, KC * (i + 1))
                    for m in range(MO):
                        bank = i % 4 if recurrence else m
                        if i and not recurrence:
                            pe.wait_ge(lo_ready, MO * (i - 1) + m + 1)
                        step = 0
                        for kc in range(KC):
                            for lhsT, rhs in split3((w[0][:, kc, m * P:(m + 1) * P], w[1][:, kc, m * P:(m + 1) * P]),
                                                    (xs[0][:, kc, :], xs[1][:, kc, :])):
                                ins = pe.matmul(acc[bank][:, :], lhsT, rhs, start=(step == 0), stop=(step == 3 * KC - 1))
                                step += 1
                        ins.then_inc(acc_done, 1)
                    if i + 2 < NB:
                        variance(i + 2)


def recur(nc, phase, K, aT):
    BK = TB // SN
    with Ctx(nc, phase) as c:
        a_raw = c.sb("a_raw", [S, S])
        a_half = c.sb("a_half", [S, S])
        pick = c.sb("pick", [P, S])
        th = c.sb("tanh", [S, 2, SN])
        differ = c.sb("differ", [S, SN])
        both = c.sb("both", [S, 2])
        excess = c.sb("excess", [S, 1])
        worst = c.sb("worst", [1, 1])
        alike = c.sb("alike", [1, 1], mybir.dt.int32)
        z = c.bank("z", SL // BK)
        flip = c.bank("flip")
        passed = c.sem("passed")
        a_loaded, a_halved, picked = c.sem("a_loaded"), c.sem("a_halved"), c.sem("picked")
        begun, z_done, tanh_done, h_done = c.sem("begun"), c.sem("z_done"), c.sem("tanh_done"), c.sem("h_done")
        checked, excess_done, flipped, told = c.sem("checked"), c.sem("excess_done"), c.sem("flipped"), c.sem("told")
        h = K.hist[0:S]

        with nc.Block() as block:
            @block.sync
            def _(sp):
                sp.dma_start(a_raw[:, :], aT).then_inc(a_loaded, 16)
                sp.wait_ge(a_loaded, 16)

            @block.vector
            def _(dve):
                dve.wait_ge(a_loaded, 16)
                dve.tensor_scalar(a_half[:, :], a_raw[:, :], 0.5, None, ALU.mult).then_inc(a_halved, 1)
                dve.memset(h[:, 0, :, :], 0.0).then_inc(begun, 1)

                def steps(p):
                    for l in range(SL):
                        dve.wait_ge(tanh_done, SL * p + l + 1)
                        dve.scalar_tensor_tensor(out=h[:, l + 1, :, :], in0=th[:, l % 2, :], scalar=1.0,
                                                 in1=z[0:S, l * SN:(l + 1) * SN], op0=ALU.add,
                                                 op1=ALU.mult).then_inc(h_done, 1)

                def begin(p):
                    dve.wait_ge(h_done, SL * p)
                    dve.tensor_copy(h[:, 0, :, 1:SC], h[:, SL, :, 0:SC - 1]).then_inc(begun, 1)
                steps(0)
                begin(1)
                steps(1)
                dve.wait_ge(h_done, 2 * SL)
                d = differ[:, 0:B * (SC - 1)].rearrange("s (b c) -> s b c", b=B)
                dve.tensor_tensor(d, h[:, SL, :, 0:SC - 1], h[:, 0, :, 1:SC], ALU.subtract).then_inc(checked, 1)
                dve.wait_ge(checked, 1)
                dve.tensor_tensor(d, d, d, ALU.mult).then_inc(checked, 1)
                dve.wait_ge(checked, 2)
                dve.tensor_reduce(both[:, 0:1], differ[:, 0:B * (SC - 1)], AX.X, ALU.max).then_inc(checked, 1)
                dve.wait_ge(checked, 3)
                dve.tensor_tensor(d, h[:, SL, :, 0:SC - 1], h[:, SL, :, 0:SC - 1], ALU.mult).then_inc(checked, 1)
                dve.wait_ge(checked, 4)
                dve.tensor_reduce(both[:, 1:2], differ[:, 0:B * (SC - 1)], AX.X, ALU.max).then_inc(checked, 1)
                dve.wait_ge(checked, 5)
                dve.scalar_tensor_tensor(out=excess[:, :], in0=both[:, 1:2], scalar=-(ALIKE ** 2), in1=both[:, 0:1],
                                         op0=ALU.mult, op1=ALU.add).then_inc(excess_done, 1)
                dve.wait_ge(flipped, 1)
                dve.tensor_reduce(worst[:, :], flip[0:1, 0:S], AX.X, ALU.max).then_inc(checked, 1)
                dve.wait_ge(checked, 6)
                dve.tensor_scalar(alike[:, :], worst[:, :], 0.0, None, ALU.is_le).then_inc(told, 1)
                dve.wait_ge(told, 1)
                same = dve.value_load(alike[0:1, 0:1], min_val=0, max_val=1)
                with dve.If(same < 1):
                    with dve.Fori(2, SC) as p:
                        begin(p)
                        steps(p)

            @block.scalar
            def _(act):
                def steps(p):
                    for l in range(SL):
                        act.wait_ge(z_done, SL * p + l + 1)
                        act.activation(th[:, l % 2, :], z[0:S, l * SN:(l + 1) * SN], ACT.Tanh,
                                       scale=0.5).then_inc(tanh_done, 1)
                steps(0)
                steps(1)
                act.wait_ge(told, 1)
                same = act.value_load(alike[0:1, 0:1], min_val=0, max_val=1)
                with act.If(same < 1):
                    with act.Fori(2, SC) as p:
                        steps(p)

            @block.gpsimd
            def _(pool):
                c.clear_last(pool)
                pool.memset(pick[:, :], 0.0).then_inc(picked, 1)
                pool.wait_ge(picked, 1)
                pool.affine_select(out=pick[:, :], in_=pick[:, :], compare_op=ALU.not_equal, fill=1.0,
                                   base=-S, pattern=[[-1, S]], channel_multiplier=1).then_inc(picked, 1)

            @block.tensor
            def _(pe):
                def steps(p):
                    drive = K.drive[:, 0:SL, :, :].rearrange("p l b c -> p (l b c)")
                    for q in range(SL // BK):
                        wait(pe, h_done, SL * p)
                        ins = pe.matmul(z[0:S, q * TB:(q + 1) * TB], pick[:, :], drive[:, q * TB:(q + 1) * TB],
                                        start=True, stop=True)
                    for l in range(SL):
                        if l == 0:
                            wait_apart(pe, begun, p + 1, passed)
                        else:
                            wait_apart(pe, h_done, SL * p + l, passed)
                        pe.matmul(z[0:S, l * SN:(l + 1) * SN], a_half[:, :], h[:, l, :, :].rearrange("s b c -> s (b c)"),
                                  start=False, stop=True, skip_group_check=True).then_inc(z_done, 1)
                pe.wait_ge(a_halved, 1)
                pe.wait_ge(picked, 2)
                steps(0)
                steps(1)
                pe.wait_ge(excess_done, 1)
                pe.transpose(flip[0:1, 0:S], excess[:, :], K.ident[0:S, 0:S]).then_inc(flipped, 1)
                pe.wait_ge(told, 1)
                same = pe.value_load(alike[0:1, 0:1], min_val=0, max_val=1)
                with pe.If(same < 1):
                    with pe.Fori(2, SC) as p:
                        steps(p)


def give_out(nc, phase, K, cmat, x3, out):
    NB = B * QB
    RING = 4
    with Ctx(nc, phase) as c:
        c_raw = c.sb("c_raw", [S, D])
        c_both = c.sb("c_both", [P, D], F32R)
        c_low = c.sb("c_low", [P, D], F32R)
        states = c.sb("states", [S, B, NQ])
        s_both = c.sb("s_both", [P, B, NQ], F32R)
        x_sb = c.sb("x", [P, 2, KC, TB])
        y = c.sb("y", [P, RING, TB])
        acc = [c.bank(f"acc{i}") for i in range(RING)]
        c_loaded, c_cleared, c_split = c.sem("c_loaded"), c.sem("c_cleared"), c.sem("c_split")
        loaded = [c.sem(f"loaded{i}") for i in range(2)]
        summed, rounded, s_split = c.sem("summed"), c.sem("rounded"), c.sem("s_split")
        acc_done, y_ready = c.sem("acc_done"), c.sem("y_ready")
        stored = [c.sem(f"stored{i}") for i in range(RING)]
        with nc.Block() as block:
            @block.sync
            def _(sp):
                sp.dma_start(c_raw[:, :], cmat).then_inc(c_loaded, 16)

                def load(i):
                    sp.dma_start(x_sb[:, i % 2], x3[:, :, i, :]).then_inc(loaded[i % 2], 16)
                load(0)
                load(1)
                for i in range(NB):
                    for m in range(KC):
                        sp.wait_ge(y_ready, KC * i + m + 1)
                        sp.dma_start(out[:, m, i, :], y[:, m, :]).then_inc(stored[m], 16)
                    if i + 2 < NB:
                        load(i + 2)
                for m in range(KC):
                    sp.wait_ge(stored[m], 16 * NB)

            @block.gpsimd
            def _(pool):
                c.clear_last(pool)
                pool.memset(c_low[S:P, :].bitcast(F32), 0.0).then_inc(c_cleared, 1)

            @block.vector
            def _(dve):
                for b in range(B):
                    dve.scalar_tensor_tensor(out=states[:, b, :].rearrange("s (c l) -> s l c", l=SL),
                                             in0=K.hist[0:S, 1:SL + 1, b, :], scalar=0.5, in1=K.drive[0:S, 1:SL + 1, b, :],
                                             op0=ALU.mult, op1=ALU.add).then_inc(summed, 1)
                for b in range(B):
                    dve.wait_ge(summed, b + 1)
                    dve.tensor_copy(s_both[0:S, b, :], states[:, b, :]).then_inc(rounded, 1)
                    dve.wait_ge(rounded, b + 1)
                    dve.tensor_tensor(s_both[S:P, b, :], states[:, b, :], s_both[0:S, b, :].bitcast(F32),
                                      ALU.subtract).then_inc(s_split, 1)
                dve.wait_ge(c_loaded, 16)
                dve.tensor_copy(c_both[0:S, :], c_raw[:, :]).then_inc(c_split, 1)
                dve.tensor_copy(c_both[S:P, :], c_raw[:, :]).then_inc(c_split, 1)
                dve.wait_ge(c_split, 1)
                dve.tensor_tensor(c_low[0:S, :], c_raw[:, :], c_both[0:S, :].bitcast(F32), ALU.subtract).then_inc(c_split, 1)
                for i in range(NB):
                    dve.wait_ge(loaded[i % 2], 16 * (i // 2 + 1))
                    for m in range(KC):
                        dve.wait_ge(acc_done, KC * i + m + 1)
                        if i:
                            dve.wait_ge(stored[m], 16 * i)
                        dve.scalar_tensor_tensor(out=y[:, m, :], in0=acc[m][:, :], scalar=K.mod[:, m, i // QB:i // QB + 1],
                                                 in1=x_sb[:, i % 2, m, :], op0=ALU.add, op1=ALU.add).then_inc(y_ready, 1)

            @block.tensor
            def _(pe):
                pe.wait_ge(c_cleared, 1)
                pe.wait_ge(c_split, 3)
                for i in range(NB):
                    b, t0 = i // QB, i % QB * TB
                    pe.wait_ge(s_split, b + 1)
                    for m in range(KC):
                        if i:
                            pe.wait_ge(y_ready, KC * (i - 1) + m + 1)
                        pe.matmul(acc[m][:, :], c_both[:, m * P:(m + 1) * P], s_both[:, b, t0:t0 + TB], start=True, stop=False)
                        pe.matmul(acc[m][:, :], c_low[:, m * P:(m + 1) * P], s_both[:, b, t0:t0 + TB],
                                  start=False, stop=True).then_inc(acc_done, 1)


def build(nc, A):
    def scratch(name, shape, dt=F32):
        return nc.dram_tensor(name, shape, dt, kind="Internal").ap()

    k0_hi, k0_lo = (scratch(f"k0_{x}", [P, KC, B * KB, TB]) for x in ("hi", "lo"))
    k1_hi, k1_lo = (scratch(f"k1_{x}", [P, KC, B * KB, TB]) for x in ("hi", "lo"))
    q0_hi, q0_lo = (scratch(f"q0_{x}", [P, KC, B * QB, TB]) for x in ("hi", "lo"))
    q1_hi, q1_lo, a1_hi, a1_lo = (scratch(n, [P, KC, B * QB, TB]) for n in ("q1_hi", "q1_lo", "a1_hi", "a1_lo"))
    a0_hi, a0_lo = (scratch(f"a0_{x}", [P, KC, B * QB, TB]) for x in ("hi", "lo"))
    x1, x2, x3 = (scratch(f"x{n}", [P, KC, B * QB, TB]) for n in (1, 2, 3))
    v0, v1 = (scratch(f"v{n}", [B * KB, P, RT, D]) for n in range(2))

    def w_view(ap):
        return ap.rearrange("(c p) o -> p c o", p=P)
    wq0 = Weight("wq0", w_view(A["wq0T"]), "ln_q_g", "ln_q_b", None, 0)
    wk0 = Weight("wk0", w_view(A["wkv0T"][:, 0:D]), "ln_kv_g", "ln_kv_b", None, KC)
    wv0 = Weight("wv0", w_view(A["wkv0T"][:, D:2 * D]), "ln_kv_g", "ln_kv_b", None, 2 * KC)
    wk1 = Weight("wk1", w_view(A["wqkv1T"][:, D:2 * D]), "g1", "beta1", "bk", 3 * KC)
    wv1 = Weight("wv1", w_view(A["wqkv1T"][:, 2 * D:3 * D]), "g1", "beta1", "bv", 4 * KC)
    with ExitStack() as stack:
        K = Kept(nc, stack)
        Ctx.last = None
        setup(nc, A, K)
        ctx_rows = A["ctx"].rearrange("b (n t p) d -> (b n) p t d", p=P, t=RT)
        x_rows = A["x"].rearrange("b (n t p) d -> (b n) p t d", p=P, t=RT)
        normalize_and_project(nc, "ctx", K, ctx_rows, B * KB, [(wv0, v0), (wv1, v1)],
                              [(wk0, k0_hi, k0_lo), (wk1, k1_hi, k1_lo)])
        normalize_and_project(nc, "xq", K, x_rows, B * QB, [], [(wq0, q0_hi, q0_lo)])
        attention(nc, "att0", K, LAYER0, (k0_hi, k0_lo), (q0_hi, q0_lo), v0, (a0_hi, a0_lo), list(range(QB)),
                  K.bias_of(wv0, 0, KC))
        project_and_add(nc, "out0", K, w_view(A["wo0T"]), (a0_hi, a0_lo), A["xT"], K.col("bo", 0, KC), x1)
        feed_forward(nc, "ffn", K, w_view(A["w1T"]), w_view(A["w2T"]), x1, x2)
        normalize_features(nc, "q1", K, x2, "g1", "beta1", w_view(A["wqkv1T"][:, 0:D]), "bq", 5 * KC, (q1_hi, q1_lo))
        attention(nc, "att1", K, LAYER1, (k1_hi, k1_lo), (q1_hi, q1_lo), v1, (a1_hi, a1_lo), list(range(QB)),
                  K.bias_of(wv1, 0, KC))
        project_and_add(nc, "out1", K, w_view(A["wo1T"]), (a1_hi, a1_lo), x2, K.col("b_o", 0, KC), x3)
        normalize_features(nc, "drive", K, x3, "g2", "beta2", None, None, 6 * KC, None,
                           recurrence={n: A[n] for n in ("w_in", "bmat", "aT")})
        recur(nc, "recur", K, A["aT"])
        give_out(nc, "give", K, A["cmat"], x3, A["outT"])
        Ctx.last[1].close()


def layout(inputs):
    import numpy as np
    g = {k: np.asarray(v) for k, v in inputs.items()}
    def T(a):
        return np.ascontiguousarray(a.T)
    bqkv = g["L1_xattn_b_qkv"]
    vec = {"ln_q_g": g["L0_xattn_ln_q_g"], "ln_q_b": g["L0_xattn_ln_q_b"], "ln_kv_g": g["L0_xattn_ln_kv_g"],
           "ln_kv_b": g["L0_xattn_ln_kv_b"], "bo": g["L0_xattn_bo"], "b1": g["L0_xattn_b1"], "b2": g["L0_xattn_b2"],
           "g1": g["L1_xattn_g1"], "beta1": g["L1_xattn_beta1"], "g2": g["L1_xattn_g2"], "beta2": g["L1_xattn_beta2"],
           "b_in": g["L1_xattn_b_in"], "bq": bqkv[0:D], "bk": bqkv[D:2 * D], "bv": bqkv[2 * D:3 * D],
           "b_o": g["L1_xattn_b_o"], "b_prog": g["L1_xattn_b_prog"]}
    cols = np.concatenate([vec[name].reshape(n, P) for name, n in VECTORS], axis=0)
    return {
        "x": g["x"], "xT": g["x"].reshape(B * QB, TB, KC, P).transpose(3, 2, 0, 1), "ctx": g["ctx_1024"],
        "probsT": g["ctxb_2048x64"].transpose(0, 2, 1), "cols": T(cols),
        "wq0T": T(g["L0_xattn_Wq"]), "wkv0T": T(g["L0_xattn_Wkv"]), "wo0T": T(g["L0_xattn_Wo"]),
        "w1T": T(g["L0_xattn_W1"]), "w2T": T(g["L0_xattn_W2"]),
        "wqkv1T": T(g["L1_xattn_W_qkv"]), "wo1T": T(g["L1_xattn_W_o"]), "w_in": g["L1_xattn_W_in"],
        "bmat": g["L1_xattn_Bmat"], "aT": T(g["L1_xattn_A"]), "cmat": g["L1_xattn_Cmat"],
        "wprogT": T(g["L1_xattn_W_prog"]),
    }


def kernel(**inputs):
    import numpy as np
    import concourse.bacc as bacc
    from concourse.bass_utils import run_bass_kernel_spmd

    nc = bacc.Bacc("TRN2", target_bir_lowering=False, num_devices=1)
    arrays, A = {}, {}
    for name, a in layout(inputs).items():
        a = np.ascontiguousarray(a)
        arrays[name] = a
        A[name] = nc.dram_tensor(name, a.shape, mybir.dt.from_np(a.dtype), kind="ExternalInput").ap()
    A["outT"] = nc.dram_tensor("outT", (P, KC, B * QB, TB), F32, kind="ExternalOutput").ap()
    build(nc, A)
    r = run_bass_kernel_spmd(nc, [arrays], core_ids=[0])
    return np.ascontiguousarray(r.results[0]["outT"].transpose(2, 3, 1, 0).reshape(B, NQ, D))
```
